# Optimizing a Trainium2 kernel written in Bass

```python
import numpy as np
import jax
import jax.numpy as jnp

def _softmax(x, axis=-1):
    return jax.nn.softmax(x, axis=axis)

def _gelu(x):
    return jax.nn.gelu(x, approximate=True)

def _silu(x):
    return jax.nn.silu(x)

def _sigmoid(x):
    return jax.nn.sigmoid(x)

def _layernorm(x, axis=-1, eps=1e-05):
    m = jnp.mean(x, axis=axis, keepdims=True)
    v = jnp.var(x, axis=axis, keepdims=True)
    return (x - m) / jnp.sqrt(v + eps)

def _scatter_add(tgt, idx, src, axis=0):
    return tgt.at[idx].add(src)

def _segment_sum(src, seg, n):
    return jax.ops.segment_sum(src, seg, n)
kernel_name = 'mk_seq_postln_d1_jaxref_r8_e00cc0'

def setup_inputs(seed: int=0):
    np.random.seed(seed)
    _w = jnp.asarray

    def _L0_attn_setup():
        import jax, jax.numpy as jnp
        import numpy as np
        B, S, E, H, WIN = (2, 256, 128, 16, 16)
        D = E // H
        key = jax.random.key(seed)
        ks = jax.random.split(key, 9)
        s = 0.02
        f32 = jnp.float32
        return {'hidden_states': jax.random.normal(ks[0], (B, S, E), f32), 'in_w_cls': jax.random.normal(ks[1], (3 * E, E), f32) * s, 'in_b_cls': jnp.zeros((3 * E,), f32), 'out_w_cls': jax.random.normal(ks[2], (E, E), f32) * s, 'out_b_cls': jnp.zeros((E,), f32), 'in_w_loc': jax.random.normal(ks[3], (3 * E, E), f32) * s, 'in_b_loc': jnp.zeros((3 * E,), f32), 'out_w_loc': jax.random.normal(ks[4], (E, E), f32) * s, 'out_b_loc': jnp.zeros((E,), f32)}
    _L0_attn_in = _L0_attn_setup()

    def _L0_ffn_setup():
        import jax, jax.numpy as jnp
        import numpy as np
        B, S, H = (2, 256, 128)
        E, F, K = (64, 64, 8)
        G, TG = (8, 4)
        SCALE = 2.5
        F_SH = 64

        def _gate(x, gate_w, gate_bias):
            scores = jax.nn.sigmoid(x @ gate_w.T)
            sc = scores + gate_bias[None, :]
            T = x.shape[0]
            group_scores = jax.lax.top_k(sc.reshape(T, G, E // G), 2)[0].sum(-1)
            _, gidx = jax.lax.top_k(group_scores, TG)
            gmask = jnp.zeros((T, G), sc.dtype).at[jnp.arange(T)[:, None], gidx].set(1.0)
            smask = jnp.repeat(gmask, E // G, axis=1)
            masked = jnp.where(smask > 0, sc, -jnp.inf)
            _, tidx = jax.lax.top_k(masked, K)
            tw = jnp.take_along_axis(scores, tidx, axis=1)
            tw = tw / (tw.sum(-1, keepdims=True) + 1e-20)
            return (tidx, tw * SCALE)
        key = jax.random.key(seed)
        ks = jax.random.split(key, 9)

        def w(k, shape, fan_in):
            return jax.random.normal(k, shape, jnp.float32) / np.float32(np.sqrt(fan_in))
        return {'hidden_states': jax.random.normal(ks[0], (B, S, H), jnp.float32), 'gate_w': w(ks[1], (E, H), H), 'gate_bias': jax.random.normal(ks[2], (E,), jnp.float32) * 0.01, 'We_gate': w(ks[3], (E, H, F), H), 'We_up': w(ks[4], (E, H, F), H), 'We_down': w(ks[5], (E, F, H), F), 'Ws_gate': w(ks[6], (H, F_SH), H), 'Ws_up': w(ks[7], (H, F_SH), H), 'Ws_down': w(ks[8], (F_SH, H), F_SH)}
    _L0_ffn_in = _L0_ffn_setup()
    _d = {'L0_attn_hidden_states': _L0_attn_in['hidden_states'], 'L0_attn_in_w_cls': _L0_attn_in['in_w_cls'], 'L0_attn_in_b_cls': _L0_attn_in['in_b_cls'], 'L0_attn_out_w_cls': _L0_attn_in['out_w_cls'], 'L0_attn_out_b_cls': _L0_attn_in['out_b_cls'], 'L0_attn_in_w_loc': _L0_attn_in['in_w_loc'], 'L0_attn_in_b_loc': _L0_attn_in['in_b_loc'], 'L0_attn_out_w_loc': _L0_attn_in['out_w_loc'], 'L0_attn_out_b_loc': _L0_attn_in['out_b_loc'], 'L0_ffn_gate_w': _L0_ffn_in['gate_w'], 'L0_ffn_gate_bias': _L0_ffn_in['gate_bias'], 'L0_ffn_We_gate': _L0_ffn_in['We_gate'], 'L0_ffn_We_up': _L0_ffn_in['We_up'], 'L0_ffn_We_down': _L0_ffn_in['We_down'], 'L0_ffn_Ws_gate': _L0_ffn_in['Ws_gate'], 'L0_ffn_Ws_up': _L0_ffn_in['Ws_up'], 'L0_ffn_Ws_down': _L0_ffn_in['Ws_down']}
    _x0 = _d['L0_attn_hidden_states']
    _d['L0_attn_hidden_states'] = jax.random.normal(jax.random.fold_in(jax.random.key(seed), 1), (16, 256, 128), dtype=_x0.dtype)
    del _x0
    return _d

def reference(L0_attn_hidden_states, L0_attn_in_w_cls, L0_attn_in_b_cls, L0_attn_out_w_cls, L0_attn_out_b_cls, L0_attn_in_w_loc, L0_attn_in_b_loc, L0_attn_out_w_loc, L0_attn_out_b_loc, L0_ffn_gate_w, L0_ffn_gate_bias, L0_ffn_We_gate, L0_ffn_We_up, L0_ffn_We_down, L0_ffn_Ws_gate, L0_ffn_Ws_up, L0_ffn_Ws_down):

    def _L0_attn_ref(hidden_states, in_w_cls, in_b_cls, out_w_cls, out_b_cls, in_w_loc, in_b_loc, out_w_loc, out_b_loc):
        import jax, jax.numpy as jnp
        import numpy as np
        B, S, E, H, WIN = (2, 256, 128, 16, 16)
        D = E // H
        b, s, e = hidden_states.shape
        sq = s - 1
        scale = 1.0 / np.sqrt(D)
        wq, wk, wv = jnp.split(in_w_cls, 3, axis=0)
        bq, bk, bv = jnp.split(in_b_cls, 3, axis=0)
        q = (hidden_states[:, 0:1] @ wq.T + bq).reshape(b, 1, H, D)
        k = (hidden_states @ wk.T + bk).reshape(b, s, H, D)
        v = (hidden_states @ wv.T + bv).reshape(b, s, H, D)
        scores = jnp.einsum('bqhd,bkhd->bhqk', q * scale, k)
        attn = jax.nn.softmax(scores, axis=-1)
        ctx = jnp.einsum('bhqk,bkhd->bqhd', attn, v).reshape(b, 1, e)
        global_out = ctx @ out_w_cls.T + out_b_cls
        wq, wk, wv = jnp.split(in_w_loc, 3, axis=0)
        bq, bk, bv = jnp.split(in_b_loc, 3, axis=0)
        Q = (hidden_states[:, 1:] @ wq.T + bq).reshape(b, sq, H, D)
        K = (hidden_states @ wk.T + bk).reshape(b, s, H, D)
        V = (hidden_states @ wv.T + bv).reshape(b, s, H, D)
        qpos = jnp.arange(1, s)
        offs = jnp.arange(-WIN, WIN + 1)
        kidx = qpos[:, None] + offs[None, :]
        valid = (kidx >= 1) & (kidx < s)
        kidx_c = jnp.clip(kidx, 0, s - 1)
        Kw = K[:, kidx_c]
        Vw = V[:, kidx_c]
        scores = jnp.einsum('bqhd,bqwhd->bhqw', Q * scale, Kw)
        scores = jnp.where(valid[None, None, :, :], scores, -1e+30)
        attn = jax.nn.softmax(scores, axis=-1)
        ctx = jnp.einsum('bhqw,bqwhd->bqhd', attn, Vw).reshape(b, sq, e)
        local_out = ctx @ out_w_loc.T + out_b_loc
        return jnp.concatenate([global_out, local_out], axis=1)

    def _L0_ffn_ref(hidden_states, gate_w, gate_bias, We_gate, We_up, We_down, Ws_gate, Ws_up, Ws_down):
        import jax, jax.numpy as jnp
        import numpy as np
        B, S, H = (2, 256, 128)
        E, F, K = (64, 64, 8)
        G, TG = (8, 4)
        SCALE = 2.5
        F_SH = 64

        def _gate(x, gate_w, gate_bias):
            scores = jax.nn.sigmoid(x @ gate_w.T)
            sc = scores + gate_bias[None, :]
            T = x.shape[0]
            group_scores = jax.lax.top_k(sc.reshape(T, G, E // G), 2)[0].sum(-1)
            _, gidx = jax.lax.top_k(group_scores, TG)
            gmask = jnp.zeros((T, G), sc.dtype).at[jnp.arange(T)[:, None], gidx].set(1.0)
            smask = jnp.repeat(gmask, E // G, axis=1)
            masked = jnp.where(smask > 0, sc, -jnp.inf)
            _, tidx = jax.lax.top_k(masked, K)
            tw = jnp.take_along_axis(scores, tidx, axis=1)
            tw = tw / (tw.sum(-1, keepdims=True) + 1e-20)
            return (tidx, tw * SCALE)
        b, s, h = hidden_states.shape
        x = hidden_states.reshape(-1, h).astype(jnp.float32)
        tidx, tw = _gate(x, gate_w, gate_bias)
        T = x.shape[0]
        w_dense = jnp.zeros((T, E), tw.dtype).at[jnp.arange(T)[:, None], tidx].add(tw)

        def body(acc, ws):
            wg, wu, wdn, cw = ws
            hmid = jax.nn.silu(x @ wg) * (x @ wu)
            return (acc + cw[:, None] * (hmid @ wdn), None)
        y, _ = jax.lax.scan(body, jnp.zeros_like(x), (We_gate, We_up, We_down, w_dense.T))
        y = y.reshape(b, s, h)
        shared = jax.nn.silu(hidden_states @ Ws_gate) * (hidden_states @ Ws_up) @ Ws_down
        return y + shared
    x = L0_attn_hidden_states
    x = _layernorm(x + _L0_attn_ref(x, L0_attn_in_w_cls, L0_attn_in_b_cls, L0_attn_out_w_cls, L0_attn_out_b_cls, L0_attn_in_w_loc, L0_attn_in_b_loc, L0_attn_out_w_loc, L0_attn_out_b_loc), axis=-1)
    x = _layernorm(x + _L0_ffn_ref(x, L0_ffn_gate_w, L0_ffn_gate_bias, L0_ffn_We_gate, L0_ffn_We_up, L0_ffn_We_down, L0_ffn_Ws_gate, L0_ffn_Ws_up, L0_ffn_Ws_down), axis=-1)
    return x

_drawn_inputs = setup_inputs


def setup_inputs(seed=0):
    import zlib

    import numpy as np

    out = dict(_drawn_inputs(seed))
    spreads = {'L0_attn_in_b_cls': (0.0, 0.8),
     'L0_attn_out_b_cls': (0.0, 2.0),
     'L0_attn_in_b_loc': (0.0, 0.1),
     'L0_attn_out_b_loc': (0.0, 0.1)}
    factors = {'L0_attn_in_w_cls': 8.0, 'L0_attn_out_w_cls': 8.0}
    for name, (base, spread) in spreads.items():
        noise = np.random.default_rng([zlib.crc32(name.encode()), seed]).standard_normal(out[name].shape)
        drawn = base * np.exp(spread * noise) if base else spread * noise
        out[name] = jnp.asarray(drawn.astype(out[name].dtype))
    for name, factor in factors.items():
        out[name] = (out[name] * factor).astype(out[name].dtype)
    return out
```

```python
import numpy as np
import concourse.bass as bass
from concourse import mybir
from contextlib import ExitStack

P = 128
BATCH, SEQ, E = 16, 256, 128
HEADS, DH, WIN = 16, 8, 16
NG, GH = 4, 4
TOK = BATCH * SEQ
NT = SEQ // P
QT = P - 2 * WIN
QN = [QT, QT, SEQ - 2 * QT]
NW = len(QN)
XW = QT * (NW - 1) + P
EXP, F, TOPK, NGRP, TOPG = 64, 64, 8, 8, 4
GS = EXP // NGRP
NPAIR = EXP // 2 + 1
QUARTERS = 4
QTOK = TOK // QUARTERS
SUB = 512
NSUB = QTOK // SUB
NEG = -1e30
EPS = 1e-5
ROUTE_SCALE = 2.5
SM_SCALE = 1.0 / float(np.sqrt(DH))

C_ID = 0
C_MQ = C_ID + P
C_MT = C_MQ + NW * P
C_SELM = C_MT + NW * QT
C_HEAD = C_SELM + NG * P
C_J = C_HEAD + HEADS
C_TOK = C_J + EXP + 2
C_C = C_TOK + NT * P
C_TRI = C_C + 3
C_N = C_TRI + NGRP * NGRP
B_QK, B_V, B_O, B_N = 0, 8 * P, 9 * P, 10 * P
W_QK = 0
W_V = W_QK + 8 * P
W_O, W_OC, W_QC, W_KC, W_VC = (W_V + P * n for n in range(1, 6))
W_G = W_VC + P
W_BQC, W_BKC, W_BVC = W_G + EXP, W_G + EXP + 1, W_G + EXP + 2
W_N = W_BVC + 1


def build(nc, x, wsmall, brows, gbias, wexp, consts, out):
    f32, f32r, bf16 = mybir.dt.float32, mybir.dt.float32r, mybir.dt.bfloat16
    ALU, ACT, AX = mybir.AluOpType, mybir.ActivationFunctionType, mybir.AxisListType
    ctx = ExitStack()
    with ctx:
        def sb(name, shape, dt=f32):
            return ctx.enter_context(nc.sbuf_tensor(name, shape, dt))

        def sem(name):
            return ctx.enter_context(nc.semaphore(name))

        def hold(eng):
            eng.sem_inc(holds, 1)

        cst = sb("cst", [P, C_N])
        wts = sb("wts", [P, W_N])
        x1_all = sb("x1_all", [P, TOK // P, E])
        x1Th = sb("x1Th", [P, TOK], f32r)
        x1Tl = sb("x1Tl", [P, TOK], f32r)
        wT_all = sb("wT_all", [P, TOK], f32r)
        ident_b = sb("ident_b", [P, P], bf16)
        maskq_b = sb("maskq_b", [P, NW, P], bf16)
        maskt_b = sb("maskt_b", [P, NW, QT], bf16)
        selm_r = sb("selm_r", [P, NG, P], f32r)
        tok_r = sb("tok_r", [4, NT, P], f32r)
        brow = sb("brow", [4, B_N])
        brow_h = sb("brow_h", [4, B_N], f32r)
        brow_r = sb("brow_r", [4, B_N], f32r)
        ones_r = sb("ones_r", [2, SEQ], f32r)
        gb = sb("gb", [P, EXP])
        neg_half = sb("neg_half", [P, 4])
        ident = cst[:, C_ID:C_ID + P]
        head_mask = cst[:, C_HEAD:C_HEAD + HEADS]
        jsel = cst[:, C_J:C_J + EXP + 2]
        c_q, c_k, c_b = (cst[:, C_C + n:C_C + n + 1] for n in range(3))
        tri = cst[:, C_TRI:C_TRI + NGRP * NGRP].rearrange("p (a b) -> p a b", a=NGRP)

        xin = sb("xin", [P, NT, E])
        xT = sb("xT", [P, XW])
        hi4 = sb("hi4", [P, 2, 2 * SEQ], f32r)
        QB = sb("QB", [P, NG, SEQ], f32r)
        KP = sb("KP", [P, NG, XW], f32r)
        V = sb("V", [P, NW, HEADS, DH + 1])
        negm = sb("negm", [P, GH, 32])
        negmT = sb("negmT", [P, QT], f32r)
        Pe = sb("Pe", [P, GH, NG, QT])
        rec = sb("rec", [P, HEADS])
        ctxn = sb("ctxn", [P, HEADS, DH])
        ctxT = sb("ctxT", [P, SEQ])
        cq = sb("cq", [P, 1])
        qblk = sb("qblk", [P, HEADS])
        cqt = sb("cqt", [P, HEADS])
        cmax = sb("cmax", [HEADS, 2])
        ca = sb("ca", [HEADS, SEQ])
        csum = sb("csum", [HEADS, 2])
        cat = sb("cat", [P, NT, HEADS])
        cxb = sb("cxb", [P, HEADS])
        cmm = sb("cmm", [P, HEADS])
        cctx = sb("cctx", [P, 1])
        cpad = sb("cpad", [P, P])
        rr = sb("rr", [P, NT, E])
        st6 = sb("st6", [P, NT, 6])
        mv = sb("mv", [P, NT, 2])
        veps = sb("veps", [P, NT])
        rstd = sb("rstd", [P, NT])
        x1t = sb("x1t", [P, NT, E])
        x1Tf = sb("x1Tf", [P, SEQ])
        th = sb("th", [P, NT, EXP])
        sg = sb("sg", [P, NT, EXP])
        sc = sb("sc", [P, NT, EXP])
        g8 = sb("g8", [P, NT, NGRP, 8])
        gs = sb("gs", [P, NT, NGRP])
        gt = sb("gt", [P, NT, NGRP, NGRP])
        ge = sb("ge", [P, NT, NGRP, NGRP])
        rank = sb("rank", [P, NT, NGRP])
        gneg = sb("gneg", [P, NT, NGRP])
        msk = sb("msk", [P, NT, EXP])
        top = sb("top", [P, NT, 8])
        rep = sb("rep", [P, NT, EXP])
        sel = sb("sel", [P, NT, EXP])
        wun = sb("wun", [P, NT, EXP])
        wsum = sb("wsum", [P, NT])
        wrec = sb("wrec", [P, NT])
        wn = sb("wn", [P, NT, EXP])
        wcat = sb("wcat", [P, NT, 2, EXP], f32r)

        wraw = sb("wraw", [P, 3, 3, P])
        wh = sb("wh", [P, 3, 3, P], f32r)
        wl = sb("wl", [P, 3, 3, P], f32r)
        wsel = sb("wsel", [P, 3, 2, F], f32r)
        SG = sb("SG", [P, NSUB, SUB])
        SU = sb("SU", [P, NSUB, SUB])
        H = sb("H", [P, NSUB, SUB])
        hh = sb("hh", [P, 3, NSUB, SUB], f32r)
        hl = sb("hl", [P, 3, NSUB, SUB], f32r)
        YT = sb("YT", [P, NSUB, SUB])
        yr = sb("yr", [P, 4, E])
        yst = sb("yst", [P, 4, 6])
        ymv = sb("ymv", [P, 4, 2])
        yve = sb("yve", [P, 4])
        yrs = sb("yrs", [P, 4])
        yo = sb("yo", [P, 4, E])

        bank = [ctx.enter_context(nc.psum_tensor(f"bank{n}", [P, 512], f32)) for n in range(8)]
        bk0, bk1 = bank[0], bank[1]
        S_bk, ST_bk = bank[2:4], bank[4:6]
        bkT, bkC = bank[6], bank[7]
        G_bk, U_bk, W_bk, Y_bk = bank[0:2], bank[2:4], bank[4:6], bank[6:8]

        ld_c, ld_x, cst_ok, pool_c = sem("ld_c"), sem("ld_x"), sem("cst_ok"), sem("pool_c")
        xfree = sem("xfree")
        xT_ps, xT_sb = sem("xT_ps"), sem("xT_sb")
        qk_ps, qk_hi, qk_sb = sem("qk_ps"), sem("qk_hi"), sem("qk_sb")
        v_ps, v_sb = sem("v_ps"), sem("v_sb")
        s_ps, smax, m_ps, bkT_free, m_sb = sem("s_ps"), sem("smax"), sem("m_ps"), sem("bkT_free"), sem("m_sb")
        st_ps, expd, pv_ps, cn, cT_ps = sem("st_ps"), sem("expd"), sem("pv_ps"), sem("cn"), sem("cT_ps")
        rec_s = sem("rec_s")
        clsP, clsA, clsV = sem("clsP"), sem("clsA"), sem("clsV")
        o_ps, dveq, var_s, pw_s, x1_s = sem("o_ps"), sem("dveq"), sem("var_s"), sem("pw_s"), sem("x1_s")
        x1T_ps, x1T_sb, g_ps, th_s, wc_s, w_ps, wT_s = (sem(n) for n in (
            "x1T_ps", "x1T_sb", "g_ps", "th_s", "wc_s", "w_ps", "wT_s"))
        x1c_s, x1l_s = sem("x1c_s"), sem("x1l_s")
        holds = sem("holds")
        ld_w, wh_s, wl_s, wsel_s = sem("ld_w"), sem("wh_s"), sem("wl_s"), sem("wsel_s")
        g_ps2, u_ps, w_b, sg_s, su_s, h_s, hh_s, hl_s, y_ps = (sem(n) for n in (
            "g_ps2", "u_ps", "w_b", "sg_s", "su_s", "h_s", "hh_s", "hl_s", "y_ps"))
        yT_s, yt_ps, yrr, yvar, ypw, yo_s, st_o = (sem(n) for n in (
            "yT_s", "yt_ps", "yrr", "yvar", "ypw", "yo_s", "st_o"))

        block = ctx.enter_context(nc.Block())

        NQ = 4
        NS = NW * GH
        TRIOS = NPAIR // 3
        DVQ = 34

        @block.sync
        def _(sp):
            sp.dma_start(cst[:], consts).then_inc(ld_c, 16)
            sp.dma_start(wts[:], wsmall).then_inc(ld_c, 16)
            sp.dma_start(brow[:], brows).then_inc(ld_c, 16)
            sp.dma_start(gb[:], gbias.partition_broadcast(P)).then_inc(ld_c, 16)
            xv = x.rearrange("(b t p) e -> b p t e", t=NT, p=P)
            with sp.Fori(0, BATCH) as b:
                sp.wait_ge(xfree, b + 1)
                hold(sp)
                sp.dma_start(xin[:], xv[b]).then_inc(ld_x, 16)

            def load(j, n, pair):
                sp.wait_ge(wl_s, n)
                hold(sp)
                sp.wait_ge(ld_w, 16 * n)
                hold(sp)
                sp.dma_start(wraw[:, (j + 1) % 3], wexp[pair]).then_inc(ld_w, 16)

            ov = out.rearrange("(q t p) e -> q p t e", t=SUB // P, p=P)
            sp.dma_start(wraw[:, 0], wexp[0]).then_inc(ld_w, 16)
            with sp.Fori(0, QUARTERS) as q:
                with sp.Fori(0, TRIOS) as k:
                    for j in range(3):
                        load(j, q * NPAIR + 3 * k + j + 1, 3 * k + j + 1)
                for s in range(NSUB):
                    sp.wait_ge(yo_s, q * NSUB + s + 1)
                    hold(sp)
                    sp.dma_start(ov[q * NSUB + s], yo[:]).then_inc(st_o, 16)
            sp.wait_ge(st_o, 16 * QUARTERS * NSUB + 16)

        @block.gpsimd
        def _(pool):
            pool.memset(ones_r[:].bitcast(f32), 1.0).then_inc(pool_c, 1)
            pool.memset(xT[:], 0.0).then_inc(pool_c, 1)
            pool.memset(KP[:].bitcast(f32), 0.0).then_inc(pool_c, 1)
            pool.memset(V[:], 1.0).then_inc(pool_c, 1)
            pool.memset(negm[:], 0.0).then_inc(pool_c, 1)
            pool.memset(ctxT[:], 0.0).then_inc(pool_c, 1)
            pool.memset(cpad[:], 0.0).then_inc(pool_c, 1)
            pool.memset(neg_half[:], -0.5).then_inc(pool_c, 1)
            pool.sem_inc(x1c_s, 1)
            pool.wait_ge(pool_c, 8)
            with pool.Fori(0, BATCH) as b:
                pool.wait_ge(var_s, b + 1)
                pool.tensor_tensor(rstd[:], veps[:], neg_half[:, 0:NT], ALU.pow).then_inc(pw_s, 1)
                pool.wait_ge(x1_s, b + 1)
                pool.tensor_copy(x1_all[:, bass.ds(NT * b, NT), :], x1t[:]).then_inc(x1c_s, 1)
                pool.wait_ge(x1T_sb, 2 * b + 2)
                pool.tensor_tensor(x1Tl[:, bass.ds(SEQ * b, SEQ)], x1Tf[:],
                                   x1Th[:, bass.ds(SEQ * b, SEQ)].bitcast(f32),
                                   ALU.subtract).then_inc(x1l_s, 1)

            def low_part(j, n, pair):
                pool.wait_ge(wh_s, n + 1)
                if pair is not None:
                    pool.tensor_copy(wsel[:, j], jsel[:, bass.ds(2 * pair, 2)].unsqueeze(2)
                                     .broadcast_to((P, 2, F))).then_inc(wsel_s, 1)
                pool.tensor_tensor(wl[:, j], wraw[:, j], wh[:, j].bitcast(f32), ALU.subtract).then_inc(wl_s, 1)

            def low_hidden(j, s, n):
                pool.wait_ge(hh_s, NSUB * n + s + 1)
                pool.tensor_tensor(hl[:, j, s], H[:, s], hh[:, j, s].bitcast(f32),
                                   ALU.subtract).then_inc(hl_s, 1)

            pool.sem_inc(wl_s, 2)
            pool.sem_inc(hl_s, 2)
            low_part(0, 0, None)
            with pool.Fori(0, QUARTERS) as q:
                with pool.Fori(0, TRIOS) as k:
                    for j in range(3):
                        n = q * NPAIR + 3 * k + j
                        low_part((j + 1) % 3, n + 1, 3 * k + j)
                        for s in range(NSUB):
                            low_hidden(j, s, n)
                for s in range(NSUB):
                    pool.wait_ge(yvar, q * NSUB + s + 1)
                    pool.tensor_tensor(yrs[:], yve[:], neg_half[:], ALU.pow).then_inc(ypw, 1)

        @block.scalar
        def _(act):
            act.wait_ge(ld_c, 64)
            act.activation(ident_b[:], ident, ACT.Copy).then_inc(cst_ok, 1)
            act.activation(maskq_b[:].rearrange("p w k -> p (w k)"), cst[:, C_MQ:C_MQ + NW * P], ACT.Copy).then_inc(cst_ok, 1)
            act.activation(maskt_b[:].rearrange("p w k -> p (w k)"), cst[:, C_MT:C_MT + NW * QT], ACT.Copy).then_inc(cst_ok, 1)
            act.activation(selm_r[:].rearrange("p w k -> p (w k)"), cst[:, C_SELM:C_SELM + NG * P], ACT.Copy).then_inc(cst_ok, 1)
            act.activation(tok_r[:].rearrange("p w k -> p (w k)"), cst[0:4, C_TOK:C_TOK + NT * P], ACT.Copy).then_inc(cst_ok, 1)
            act.activation(brow_h[:], brow[:], ACT.Copy).then_inc(cst_ok, 1)
            act.preload_act_table(ACT.Exp)
            act.sem_inc(expd, 2)
            act.sem_inc(bkT_free, 1)
            act.sem_inc(th_s, 1)
            act.sem_inc(wT_s, 1)
            with act.Fori(0, BATCH) as b:
                act.wait_ge(xT_ps, b + 1)
                act.activation(xT[:, WIN:WIN + SEQ], bk0[:, 0:SEQ], ACT.Copy).then_inc(xT_sb, 1)
                for k in range(NQ):
                    act.wait_ge(qk_ps, NQ * b + k + 1)
                    act.activation(hi4[:, k % 2], bank[1 - k % 2][:], ACT.Copy).then_inc(qk_hi, 1)
                act.wait_ge(v_ps, b + 1)
                act.activation(V[:, :, :, 0:DH], bk1[:, 0:NW * P].rearrange("p (w h d) -> p w h d", w=NW, h=HEADS),
                               ACT.Copy).then_inc(v_sb, 1)
                act.wait_ge(clsP, 6 * b + 1)
                act.activation(cq[:], bk0[:, 0:1], ACT.Identity, bias=wts[:, W_BQC:W_BQC + 1]).then_inc(clsA, 1)

                def max_row(t):
                    act.wait_ge(m_ps, NW * b + t + 1)
                    act.activation(negmT[:, 0:QN[t]], bkT[:, 0:QN[t]], ACT.Copy).then_inc(bkT_free, 1)

                def exps(t):
                    for r in range(GH):
                        act.wait_ge(st_ps, NS * b + GH * t + r + 1)
                        act.activation(Pe[:, r, :, 0:QN[t]],
                                       ST_bk[r % 2][:, 0:NG * QN[t]].rearrange("p (g q) -> p g q", g=NG),
                                       ACT.Exp, scale=SM_SCALE).then_inc(expd, 1)

                def ctx_rows(t):
                    act.wait_ge(cT_ps, NW * b + t + 1)
                    lo = 1 if t == 0 else 0
                    act.activation(ctxT[:, QT * t + lo:QT * t + QN[t]], bkT[:, lo:QN[t]],
                                   ACT.Copy).then_inc(bkT_free, 1)

                max_row(0)
                exps(0)
                act.wait_ge(clsV, 7 * b + 3)
                act.activation(ca[:], bk0[0:HEADS, 0:SEQ], ACT.Exp, bias=cmax[:, 1:2], scale=SM_SCALE,
                               accum_out=csum[:, 0:1]).then_inc(clsA, 1)
                max_row(1)
                exps(1)
                ctx_rows(0)
                max_row(2)
                exps(2)
                ctx_rows(1)
                ctx_rows(2)
                act.wait_ge(x1T_ps, b + 1)
                act.activation(x1Tf[:], bk0[:, 0:SEQ], ACT.Copy).then_inc(x1T_sb, 1)
                act.activation(x1Th[:, bass.ds(SEQ * b, SEQ)], bk0[:, 0:SEQ], ACT.Copy).then_inc(x1T_sb, 1)
                act.wait_ge(g_ps, b + 1)
                act.activation(th[:].rearrange("p j e -> p (j e)"), bk1[:, 0:NT * EXP], ACT.Tanh, scale=0.5).then_inc(th_s, 1)
                act.wait_ge(w_ps, b + 1)
                act.activation(wT_all[:, bass.ds(SEQ * b, SEQ)], bk0[:, 0:SEQ], ACT.Copy).then_inc(wT_s, 1)

            act.preload_act_table(ACT.Silu)
            act.sem_inc(sg_s, 2)
            act.sem_inc(yT_s, 2)

            def high_part(j, n):
                act.wait_ge(ld_w, 16 * n + 16)
                act.wait_ge(y_ps, NSUB * n + 1)
                act.activation(wh[:, j], wraw[:, j], ACT.Copy).then_inc(wh_s, 1)

            def hidden(s, n):
                act.wait_ge(g_ps2, NSUB * n + s + 1)
                act.wait_ge(su_s, NSUB * n + s + 1)
                act.activation(SG[:, s], G_bk[s][:], ACT.Silu).then_inc(sg_s, 1)

            def high_hidden(j, s, n):
                act.wait_ge(h_s, NSUB * n + s + 3)
                act.activation(hh[:, j, s], H[:, s], ACT.Copy).then_inc(hh_s, 1)

            high_part(0, 0)
            with act.Fori(0, QUARTERS) as q:
                with act.Fori(0, TRIOS) as k:
                    for j in range(3):
                        n = q * NPAIR + 3 * k + j
                        hidden(0, n)
                        high_part((j + 1) % 3, n + 1)
                        hidden(1, n)
                        high_hidden(j, 0, n)
                        high_hidden(j, 1, n)
                for s in range(NSUB):
                    act.wait_ge(y_ps, NSUB * (q + 1) * NPAIR + s + 4)
                    act.activation(YT[:, s], Y_bk[s][:], ACT.Copy).then_inc(yT_s, 1)

        @block.vector
        def _(dve):
            links = [0]

            def link(ins, base):
                links[0] += 1
                ins.then_inc(dveq, 1)
                dve.wait_ge(dveq, base + links[0])

            dve.wait_ge(cst_ok, 6)
            dve.scalar_tensor_tensor(brow_r[:], brow_h[:].bitcast(f32), c_b[0:4], brow[:],
                                     ALU.mult, ALU.add).then_inc(cst_ok, 1)
            dve.wait_ge(pool_c, 8)
            dve.sem_inc(smax, 2)
            dve.sem_inc(cn, 1)
            dve.sem_inc(xfree, 1)
            with dve.Fori(0, BATCH) as b:
                links[0] = 0
                base = DVQ * b
                for k in range(NQ):
                    dve.wait_ge(qk_hi, NQ * b + k + 1)
                    g = 2 * (k % 2)
                    dst, c = (QB[:, g:g + 2, :], c_q) if k < 2 else (KP[:, g:g + 2, WIN:WIN + SEQ], c_k)
                    dve.scalar_tensor_tensor(dst, hi4[:, k % 2].bitcast(f32).rearrange("p (a s) -> p a s", a=2), c,
                                             bank[1 - k % 2][:].rearrange("p (a s) -> p a s", a=2),
                                             ALU.mult, ALU.add).then_inc(qk_sb, 1)
                dve.wait_ge(clsA, 2 * b + 1)
                dve.tensor_scalar(qblk[:], head_mask, cq[:, 0:1], None, ALU.mult).then_inc(clsV, 1)

                def maxima(t):
                    n = QN[t]
                    for r in range(GH):
                        dve.wait_ge(s_ps, NS * b + GH * t + r + 1)
                        dve.tensor_reduce(negm[0:n, r, 0:NG],
                                          S_bk[r % 2][0:n, :].rearrange("p (g k) -> p g k", g=NG),
                                          AX.X, ALU.max, negate=True).then_inc(smax, 1)

                def normalise(t):
                    n = QN[t]
                    cv = bkC[0:n, 0:HEADS * (DH + 1)].rearrange("p (h d) -> p h d", h=HEADS)
                    dve.wait_ge(pv_ps, NW * b + t + 1)
                    link(dve.reciprocal(rec[0:n], cv[:, :, DH]), base)
                    dve.tensor_tensor(ctxn[0:n], cv[:, :, 0:DH],
                                      rec[0:n].unsqueeze(2).broadcast_to((n, HEADS, DH)), ALU.mult).then_inc(cn, 1)

                maxima(0)
                dve.wait_ge(clsP, 6 * b + 2)
                dve.tensor_copy(cqt[:], bk0[:, 0:HEADS]).then_inc(clsV, 1)
                maxima(1)
                dve.wait_ge(clsP, 6 * b + 3)
                link(dve.tensor_reduce(cmax[:, 0:1], bk0[0:HEADS, 0:SEQ], AX.X, ALU.max, negate=True), base)
                dve.tensor_scalar(cmax[:, 1:2], cmax[:, 0:1], SM_SCALE, None, ALU.mult).then_inc(clsV, 1)
                normalise(0)
                maxima(2)
                dve.wait_ge(clsA, 2 * b + 2)
                link(dve.reciprocal(csum[:, 1:2], csum[:, 0:1]), base)
                dve.tensor_scalar(ca[:], ca[:], csum[:, 1:2], None, ALU.mult).then_inc(clsV, 1)
                dve.wait_ge(clsP, 6 * b + 4)
                dve.tensor_copy(cat[:].rearrange("p j h -> p (j h)"), bk0[:, 0:NT * HEADS]).then_inc(clsV, 1)
                dve.wait_ge(clsP, 6 * b + 5)
                dve.tensor_copy(cxb[:], bk0[:, 0:HEADS]).then_inc(clsV, 1)
                normalise(1)
                dve.wait_ge(clsP, 6 * b + 6)
                link(dve.tensor_tensor(cmm[:], bk0[:, 0:HEADS], head_mask, ALU.mult), base)
                link(dve.reduce_sum(cctx[:], cmm[:], AX.X), base)
                dve.tensor_tensor(cpad[:, 0:1], cctx[:], wts[:, W_BVC:W_BVC + 1], ALU.add).then_inc(clsV, 1)
                normalise(2)

                dve.wait_ge(o_ps, b + 1)
                dve.tensor_tensor(rr[:].rearrange("p j e -> p (j e)"), bk1[:, 0:NT * E],
                                  xin[:].rearrange("p j e -> p (j e)"), ALU.add).then_inc(xfree, 1)
                dve.wait_ge(xfree, b + 2)
                for j in range(NT):
                    link(dve.bn_stats(st6[:, j], rr[:, j]), base)
                for j in range(NT):
                    hold(dve)
                    link(dve.bn_aggr(mv[:, j], st6[:, j]), base)
                dve.tensor_scalar(veps[:], mv[:, :, 1], EPS, None, ALU.add).then_inc(var_s, 1)
                dve.wait_ge(pw_s, b + 1)
                dve.wait_ge(x1c_s, b + 1)
                for j in range(NT):
                    last = dve.tensor_scalar(x1t[:, j], rr[:, j], mv[:, j, 0:1], rstd[:, j:j + 1],
                                             ALU.subtract, ALU.mult)
                    if j < NT - 1:
                        link(last, base)
                last.then_inc(x1_s, 1)

                dve.wait_ge(th_s, b + 2)
                link(dve.tensor_scalar(sg[:], th[:], 0.5, 0.5, ALU.mult, ALU.add), base)
                link(dve.tensor_tensor(sc[:], sg[:], gb[:].unsqueeze(1).broadcast_to((P, NT, EXP)), ALU.add), base)
                hold(dve)
                for j in range(NT):
                    for a in range(NGRP):
                        last = dve.max(g8[:, j, a], sc[:, j, GS * a:GS * (a + 1)])
                link(last, base)
                link(dve.tensor_tensor(gs[:], g8[:, :, :, 0], g8[:, :, :, 1], ALU.add), base)
                gsb = gs[:].unsqueeze(2).broadcast_to((P, NT, NGRP, NGRP))
                gsa = gs[:].unsqueeze(3).broadcast_to((P, NT, NGRP, NGRP))
                dve.tensor_tensor(gt[:], gsb, gsa, ALU.is_gt)
                link(dve.tensor_tensor(ge[:], gsb, gsa, ALU.is_ge), base)
                link(dve.tensor_tensor(ge[:], ge[:], tri.unsqueeze(1).broadcast_to((P, NT, NGRP, NGRP)), ALU.mult), base)
                link(dve.tensor_tensor(ge[:], gt[:], ge[:], ALU.max), base)
                link(dve.reduce_sum(rank[:], ge[:], AX.X), base)
                link(dve.tensor_scalar(gneg[:], rank[:], float(TOPG), NEG, ALU.is_ge, ALU.mult), base)
                link(dve.tensor_tensor(msk[:].rearrange("p j (a s) -> p j a s", a=NGRP),
                                       sc[:].rearrange("p j (a s) -> p j a s", a=NGRP),
                                       gneg[:].unsqueeze(3).broadcast_to((P, NT, NGRP, GS)), ALU.add), base)
                for j in range(NT):
                    hold(dve)
                    link(dve.max(top[:, j], msk[:, j]), base)
                for j in range(NT):
                    hold(dve)
                    link(dve.match_replace(rep[:, j], top[:, j], msk[:, j], -3e38), base)
                link(dve.tensor_tensor(sel[:], rep[:], msk[:], ALU.not_equal), base)
                link(dve.tensor_tensor(wun[:], sg[:], sel[:], ALU.mult), base)
                link(dve.reduce_sum(wsum[:], wun[:], AX.X), base)
                link(dve.tensor_scalar(wsum[:], wsum[:], 1e-20, None, ALU.add), base)
                link(dve.reciprocal(wrec[:], wsum[:]), base)
                for j in range(NT):
                    link(dve.tensor_scalar(wn[:, j], wun[:, j], wrec[:, j:j + 1], ROUTE_SCALE, ALU.mult, ALU.mult), base)
                link(dve.tensor_copy(wcat[:, :, 0], wn[:]), base)
                dve.tensor_tensor(wcat[:, :, 1], wn[:], wcat[:, :, 0].bitcast(f32), ALU.subtract).then_inc(wc_s, 1)
            assert links[0] == DVQ, links[0]

            dve.wait_ge(x1c_s, BATCH + 1)
            dve.sem_inc(su_s, 2)
            dve.sem_inc(h_s, 2)
            dve.sem_inc(yrr, 2)
            dve.sem_inc(st_o, 16)

            def hidden(s, n, routed):
                c = NSUB * n + s
                dve.wait_ge(sg_s, c + 3)
                dve.wait_ge(u_ps, c + 1)
                dve.tensor_tensor(SU[:, s], SG[:, s], U_bk[s][:], ALU.mult).then_inc(su_s, 1)
                dve.wait_ge(su_s, c + 3)
                dve.wait_ge(hl_s, c + 1)
                if routed is None:
                    dve.tensor_copy(H[:, s], SU[:, s]).then_inc(h_s, 1)
                else:
                    dve.wait_ge(w_b, routed + s + 1)
                    dve.tensor_tensor(H[:, s], SU[:, s], W_bk[s][:], ALU.mult).then_inc(h_s, 1)

            YL = 8
            with dve.Fori(0, QUARTERS) as q:
                for s in range(NSUB):
                    hidden(s, q * NPAIR, None)
                for j in (1, 2):
                    for s in range(NSUB):
                        hidden(s, q * NPAIR + j, q * NSUB * (NPAIR - 1) + NSUB * (j - 1))
                with dve.Fori(1, TRIOS) as k:
                    for j in range(3):
                        for s in range(NSUB):
                            hidden(s, q * NPAIR + 3 * k + j,
                                   q * NSUB * (NPAIR - 1) + NSUB * 3 * (k - 1) + NSUB * (j + 2))
                links[0] = 0
                base = DVQ * BATCH + NSUB * YL * q
                for s in range(NSUB):
                    i = q * NSUB + s
                    dve.wait_ge(yt_ps, i + 1)
                    dve.tensor_tensor(yr[:], G_bk[s][:].rearrange("p (t e) -> p t e", e=E),
                                      x1_all[:, bass.ds((SUB // P) * i, SUB // P), :], ALU.add).then_inc(yrr, 1)
                    dve.wait_ge(yrr, i + 3)
                    for t in range(4):
                        link(dve.bn_stats(yst[:, t], yr[:, t]), base)
                    for t in range(4):
                        hold(dve)
                        link(dve.bn_aggr(ymv[:, t], yst[:, t]), base)
                    dve.tensor_scalar(yve[:], ymv[:, :, 1], EPS, None, ALU.add).then_inc(yvar, 1)
                    dve.wait_ge(ypw, i + 1)
                    dve.wait_ge(st_o, 16 * i + 16)
                    for t in range(4):
                        last = dve.tensor_scalar(yo[:, t], yr[:, t], ymv[:, t, 0:1], yrs[:, t:t + 1],
                                                 ALU.subtract, ALU.mult)
                    last.then_inc(yo_s, 1)
                    dve.wait_ge(yo_s, i + 1)

        @block.tensor
        def _(pe):
            def mm(o, a, b_, first, last):
                return pe.matmul(o, a, b_, start=first, stop=last)

            pe.wait_ge(cst_ok, 7)
            pe.wait_ge(pool_c, 8)
            with pe.Fori(0, BATCH) as b:
                pe.wait_ge(ld_x, 16 * b + 16)
                pe.wait_ge(wT_s, b + 1)
                for j in range(NT):
                    last = pe.transpose(bk0[:, P * j:P * (j + 1)], xin[:, j], ident)
                last.then_inc(xT_ps, 1)
                pe.wait_ge(xT_sb, b + 1)
                pe.wait_ge(th_s, b + 1)
                xq = xT[:, WIN:WIN + SEQ]
                for k in range(NQ):
                    if k >= 2:
                        pe.wait_ge(qk_sb, NQ * b + k - 1)
                    for m in range(2):
                        blk = 2 * k + m
                        o = bank[1 - k % 2][:, SEQ * m:SEQ * (m + 1)]
                        mm(o, brow_r[0:2, B_QK + P * blk:B_QK + P * (blk + 1)], ones_r[:], True, False)
                        last = mm(o, wts[:, W_QK + P * blk:W_QK + P * (blk + 1)], xq, False, True)
                    last.then_inc(qk_ps, 1)
                pe.wait_ge(qk_sb, NQ * b + NQ - 1)
                for t in range(NW):
                    o = bk1[:, P * t:P * (t + 1)]
                    mm(o, ones_r[:, 0:P], brow_r[0:2, B_V:B_V + P], True, False)
                    last = mm(o, xT[:, QT * t:QT * t + P], wts[:, W_V:W_V + P], False, True)
                last.then_inc(v_ps, 1)
                pe.wait_ge(qk_sb, NQ * b + NQ)
                mm(bk0[:, 0:1], wts[:, W_QC:W_QC + P], xT[:, WIN:WIN + 1], True, True).then_inc(clsP, 1)

                def scores(t):
                    n = QN[t]
                    for r in range(GH):
                        i = NS * b + GH * t + r
                        pe.wait_ge(smax, i + 1)
                        hold(pe)
                        o = S_bk[r % 2]
                        mm(o[0:n, :].rearrange("p (g k) -> p g k", g=NG), ident_b[0:n, 0:n],
                           maskq_b[0:n, t].unsqueeze(1).broadcast_to((n, NG, P)), True, False)
                        for g in range(NG):
                            last = mm(o[0:n, P * g:P * (g + 1)], QB[32 * r:32 * r + 32, g, QT * t:QT * t + n],
                                      KP[32 * r:32 * r + 32, g, QT * t:QT * t + P], False, g == NG - 1)
                        last.then_inc(s_ps, 1)

                def max_rows(t, k):
                    n = QN[t]
                    pe.wait_ge(smax, NS * b + GH * (t + 1) + 2)
                    pe.wait_ge(bkT_free, 2 * NW * b + k + 1)
                    hold(pe)
                    pe.transpose(bkT[:, 0:n], negm[0:n].rearrange("p r c -> p (r c)"),
                                 ident[0:n, 0:n]).then_inc(m_ps, 1)

                def scores_t(t, k):
                    n = QN[t]
                    pe.wait_ge(bkT_free, 2 * NW * b + k + 2)
                    for r in range(GH):
                        i = NS * b + GH * t + r
                        pe.wait_ge(expd, i + 1)
                        o = ST_bk[r % 2]
                        mm(o[:, 0:NG * n].rearrange("p (g q) -> p g q", g=NG), ident_b[:],
                           maskt_b[:, t, 0:n].unsqueeze(1).broadcast_to((P, NG, n)), True, False)
                        for g in range(NG):
                            rows = slice(32 * r, 32 * r + 32)
                            mm(o[:, n * g:n * (g + 1)], selm_r[rows, g], negmT[rows, 0:n], False, False)
                            last = mm(o[:, n * g:n * (g + 1)], KP[rows, g, QT * t:QT * t + P],
                                      QB[rows, g, QT * t:QT * t + n], False, g == NG - 1)
                        last.then_inc(st_ps, 1)

                def pv(t):
                    n = QN[t]
                    pe.wait_ge(cn, NW * b + t + 1)
                    for r in range(GH):
                        pe.wait_ge(expd, NS * b + GH * t + r + 3)
                        for g in range(NG):
                            h = NG * g + r
                            last = mm(bkC[0:n, (DH + 1) * h:(DH + 1) * (h + 1)], Pe[:, r, g, 0:n],
                                      V[:, t, h], True, True)
                    last.then_inc(pv_ps, 1)

                def ctx_t(t, k):
                    n = QN[t]
                    pe.wait_ge(cn, NW * b + t + 2)
                    pe.wait_ge(bkT_free, 2 * NW * b + k + 1)
                    hold(pe)
                    pe.transpose(bkT[:, 0:n], ctxn[0:n].rearrange("p h d -> p (h d)"),
                                 ident[0:n, 0:n]).then_inc(cT_ps, 1)

                scores(0)
                pe.wait_ge(clsV, 7 * b + 1)
                mm(bk0[:, 0:HEADS], wts[:, W_KC:W_KC + P], qblk[:], True, True).then_inc(clsP, 1)
                max_rows(0, 0)
                scores(1)
                pe.wait_ge(clsV, 7 * b + 2)
                mm(bk0[0:HEADS, 0:SEQ], cqt[:], xq, True, False)
                mm(bk0[0:HEADS, 0:SEQ], qblk[:], wts[:, W_BKC:W_BKC + 1].broadcast_to((P, SEQ)),
                   False, True).then_inc(clsP, 1)
                scores_t(0, 0)
                pe.wait_ge(v_sb, b + 1)
                pv(0)
                max_rows(1, 1)
                scores(2)
                pe.wait_ge(clsV, 7 * b + 4)
                hold(pe)
                for j in range(NT):
                    last = pe.transpose(bk0[:, HEADS * j:HEADS * (j + 1)], ca[:, P * j:P * (j + 1)],
                                        ident[0:HEADS, 0:HEADS])
                last.then_inc(clsP, 1)
                scores_t(1, 1)
                pe.wait_ge(clsV, 7 * b + 5)
                for j in range(NT):
                    last = mm(bk0[:, 0:HEADS], xin[:, j], cat[:, j], j == 0, j == NT - 1)
                last.then_inc(clsP, 1)
                ctx_t(0, 2)
                pv(1)
                max_rows(2, 3)
                scores_t(2, 3)
                pe.wait_ge(clsV, 7 * b + 6)
                mm(bk0[:, 0:HEADS], wts[:, W_VC:W_VC + P], cxb[:], True, True).then_inc(clsP, 1)
                ctx_t(1, 4)
                pv(2)
                ctx_t(2, 5)
                pe.wait_ge(bkT_free, 2 * NW * (b + 1) + 1)
                pe.wait_ge(clsV, 7 * b + 7)
                for j in range(NT):
                    o = bk1[:, P * j:P * (j + 1)]
                    mm(o, tok_r[:, j], brow_r[:, B_O:B_O + P], True, False)
                    if j == 0:
                        mm(o, cpad[:], wts[:, W_OC:W_OC + P], False, False)
                    last = mm(o, ctxT[:, P * j:P * (j + 1)], wts[:, W_O:W_O + P], False, True)
                last.then_inc(o_ps, 1)
                pe.wait_ge(x1_s, b + 1)
                for j in range(NT):
                    last = pe.transpose(bk0[:, P * j:P * (j + 1)], x1t[:, j], ident)
                last.then_inc(x1T_ps, 1)
                pe.wait_ge(x1T_sb, 2 * b + 2)
                for j in range(NT):
                    last = mm(bk1[:, EXP * j:EXP * (j + 1)], x1Tf[:, P * j:P * (j + 1)],
                              wts[:, W_G:W_G + EXP], True, True)
                last.then_inc(g_ps, 1)
                pe.wait_ge(wc_s, b + 1)
                for j in range(NT):
                    last = pe.transpose(bk0[:, P * j:P * (j + 1)],
                                        wcat[:, j].bitcast(f32).rearrange("p a e -> p (a e)"), ident)
                last.then_inc(w_ps, 1)

            pe.wait_ge(wT_s, BATCH + 1)
            pe.wait_ge(x1l_s, BATCH)
            pe.wait_ge(smax, NS * BATCH + 2)
            pe.wait_ge(cn, NW * BATCH + 1)
            pe.sem_inc(y_ps, 5)

            def gate_up(j, s, q, n, first):
                c = NSUB * n + s
                xs = bass.ds(QTOK * q + SUB * s, SUB)
                pe.wait_ge(sg_s, c + 1)
                if s == 0:
                    pe.wait_ge(wl_s, n + 3)
                if first:
                    pe.wait_ge(yrr, NSUB * q + s + 1)
                mm(G_bk[s][:], wh[:, j, 0], x1Th[:, xs], True, False)
                mm(G_bk[s][:], wh[:, j, 0], x1Tl[:, xs], False, False)
                mm(G_bk[s][:], wl[:, j, 0], x1Th[:, xs], False, True).then_inc(g_ps2, 1)
                pe.wait_ge(su_s, c + 1)
                mm(U_bk[s][:], wh[:, j, 1], x1Th[:, xs], True, False)
                mm(U_bk[s][:], wh[:, j, 1], x1Tl[:, xs], False, False)
                mm(U_bk[s][:], wl[:, j, 1], x1Th[:, xs], False, True).then_inc(u_ps, 1)
                if not first:
                    pe.wait_ge(h_s, c + 1)
                    if s == 0:
                        pe.wait_ge(wsel_s, n)
                    mm(W_bk[s][:], wsel[:, j].rearrange("p a f -> p (a f)"), wT_all[:, xs],
                       True, True).then_inc(w_b, 1)

            def down(j, s, q, n, first, last):
                c = NSUB * n + s
                if first:
                    pe.wait_ge(yT_s, NSUB * q + s + 1)
                pe.wait_ge(hh_s, c + 1)
                mm(Y_bk[s][:], wh[:, j, 2], hh[:, j, s], first, False)
                mm(Y_bk[s][:], wl[:, j, 2], hh[:, j, s], False, False)
                pe.wait_ge(hl_s, c + 3)
                mm(Y_bk[s][:], wh[:, j, 2], hl[:, j, s], False, last).then_inc(y_ps, 1)

            with pe.Fori(0, QUARTERS) as q:
                n0 = q * NPAIR
                for s in range(NSUB):
                    gate_up(0, s, q, n0, True)
                for j in (1, 2):
                    for s in range(NSUB):
                        gate_up(j, s, q, n0 + j, False)
                        down(j - 1, s, q, n0 + j - 1, j == 1, False)
                with pe.Fori(1, TRIOS) as k:
                    for j in range(3):
                        n = q * NPAIR + 3 * k + j
                        for s in range(NSUB):
                            gate_up(j, s, q, n, False)
                            down((j + 2) % 3, s, q, n - 1, False, False)
                for s in range(NSUB):
                    down(2, s, q, n0 + NPAIR - 1, False, True)
                for s in range(NSUB):
                    i = NSUB * q + s
                    pe.wait_ge(yT_s, i + 3)
                    pe.wait_ge(sg_s, NSUB * (n0 + NPAIR) + s + 1)
                    for t in range(SUB // P):
                        last = pe.transpose(G_bk[s][:, P * t:P * (t + 1)], YT[:, s, P * t:P * (t + 1)], ident)
                    last.then_inc(yt_ps, 1)


def layouts(a):
    def f(n):
        return np.ascontiguousarray(np.asarray(a[n]))

    e = E
    wl_, bl = f("L0_attn_in_w_loc"), f("L0_attn_in_b_loc")
    wc, bc = f("L0_attn_in_w_cls"), f("L0_attn_in_b_cls")
    ws = np.zeros((P, W_N), np.float32)
    br = np.zeros((4, B_N), np.float32)
    for part in range(2):
        for g in range(NG):
            for r in range(GH):
                h = NG * g + r
                rows = slice(part * e + DH * h, part * e + DH * (h + 1))
                for c in range(3):
                    at = P * (NG * part + g) + 32 * r + DH * c
                    ws[:, W_QK + at:W_QK + at + DH] = wl_[rows].T
                    br[0:2, B_QK + at:B_QK + at + DH] = bl[rows]
    ws[:, W_V:W_V + P] = wl_[2 * e:].T
    ws[:, W_O:W_O + P] = f("L0_attn_out_w_loc").T
    ws[:, W_OC:W_OC + P] = f("L0_attn_out_w_cls").T
    ws[:, W_QC:W_QC + P] = wc[:e].T
    ws[:, W_KC:W_KC + P] = wc[e:2 * e]
    ws[:, W_VC:W_VC + P] = wc[2 * e:].T
    ws[:, W_G:W_G + EXP] = f("L0_ffn_gate_w").T
    ws[:, W_BQC], ws[:, W_BKC], ws[:, W_BVC] = bc[:e], bc[e:2 * e], bc[2 * e:]
    br[0:2, B_V:B_V + P] = bl[2 * e:]
    br[0:2, B_O:B_O + P] = f("L0_attn_out_b_loc")
    br[2:4, B_O:B_O + P] = f("L0_attn_out_b_cls")
    we = np.zeros((NPAIR + 1, P, 3, P), np.float32)
    for at in (0, NPAIR):
        we[at, :, 0, :F], we[at, :, 1, :F], we[at, :F, 2] = f("L0_ffn_Ws_gate"), f("L0_ffn_Ws_up"), f("L0_ffn_Ws_down")
    for i, n in enumerate(("L0_ffn_We_gate", "L0_ffn_We_up")):
        we[1:NPAIR, :, i] = f(n).reshape(EXP // 2, 2, P, F).transpose(0, 2, 1, 3).reshape(EXP // 2, P, P)
    we[1:NPAIR, :, 2] = f("L0_ffn_We_down").reshape(EXP // 2, P, P)
    return {"x": f("L0_attn_hidden_states").reshape(TOK, E), "wsmall": ws, "brows": br,
            "gbias": f("L0_ffn_gate_bias"), "wexp": we, "consts": constants()}


def constants():
    c = np.zeros((P, C_N), np.float32)
    c[:, C_ID:C_ID + P] = np.eye(P)
    i, j = np.arange(QT)[:, None], np.arange(P)[None]
    for t in range(NW):
        key = QT * t - WIN + j
        ok = (j - i >= 0) & (j - i <= 2 * WIN) & (key >= 1) & (key < SEQ)
        m = np.where(ok, 0.0, NEG)
        c[0:QT, C_MQ + P * t:C_MQ + P * (t + 1)] = m
        c[:, C_MT + QT * t:C_MT + QT * (t + 1)] = m.T
    for r in range(GH):
        for g in range(NG):
            c[32 * r + g, C_SELM + P * g:C_SELM + P * (g + 1)] = 1
    c[np.arange(P), C_HEAD + np.arange(P) // DH] = 1
    c[np.arange(P), C_J + np.arange(P) % EXP] = 1
    c[0:2, C_TOK:C_TOK + NT * P] = 1
    c[0:2, C_TOK] = 0
    c[2:4, C_TOK] = 1
    rep = np.arange(P) % 32 // DH
    c[:, C_C] = np.where(rep == 1, -1, 0)
    c[:, C_C + 1] = np.where(rep == 2, -1, 0)
    c[:4, C_C + 2] = [0, -1, 0, -1]
    c[:, C_TRI:] = np.tril(np.ones((NGRP, NGRP)), -1).reshape(-1)
    return c


def kernel(**inputs):
    import concourse.bacc as _bacc
    from concourse.bass_utils import run_bass_kernel_spmd as _run

    nc = _bacc.Bacc("TRN2", target_bir_lowering=False, num_devices=1)
    arrays = layouts(inputs)
    args = [nc.dram_tensor(f"in_{n}", a.shape, mybir.dt.float32, kind="ExternalInput").ap()
            for n, a in arrays.items()]
    args.append(nc.dram_tensor("out_0", (TOK, E), mybir.dt.float32, kind="ExternalOutput").ap())
    build(nc, *args)
    r = _run(nc, [{f"in_{n}": a for n, a in arrays.items()}], core_ids=[0])
    return r.results[0]["out_0"].reshape(BATCH, SEQ, E)
```

```python
import numpy as np
import concourse.bass as bass
from concourse import mybir
from contextlib import ExitStack

P = 128
BATCH, SEQ, E = 16, 256, 128
HEADS, DH, WIN = 16, 8, 16
NG, GH = 4, 4
TOK = BATCH * SEQ
NT = SEQ // P
QT = P - 2 * WIN
QN = [QT, QT, SEQ - 2 * QT]
NW = len(QN)
XW = QT * (NW - 1) + P
EXP, F, TOPK, NGRP, TOPG = 64, 64, 8, 8, 4
GS = EXP // NGRP
NPAIR = EXP // 2 + 1
QUARTERS = 4
QTOK = TOK // QUARTERS
SUB = 512
NSUB = QTOK // SUB
NEG = -1e30
EPS = 1e-5
ROUTE_SCALE = 2.5
SM_SCALE = 1.0 / float(np.sqrt(DH))

C_ID = 0
C_MQ = C_ID + P
C_MT = C_MQ + NW * P
C_SELM = C_MT + NW * QT
C_HEAD = C_SELM + NG * P
C_J = C_HEAD + HEADS
C_TOK = C_J + EXP + 2
C_C = C_TOK + NT * P
C_N = C_C + 3
B_QK, B_V, B_O, B_N = 0, 8 * P, 9 * P, 10 * P
W_QK = 0
W_V = W_QK + 8 * P
W_O, W_OC, W_QC, W_KC, W_VC = (W_V + P * n for n in range(1, 6))
W_G = W_VC + P
W_BQC, W_BKC, W_BVC = W_G + EXP, W_G + EXP + 1, W_G + EXP + 2
W_N = W_BVC + 1


def build(nc, x, wsmall, brows, gbias, wexp, consts, out):
    f32, f32r, bf16 = mybir.dt.float32, mybir.dt.float32r, mybir.dt.bfloat16
    ALU, ACT, AX = mybir.AluOpType, mybir.ActivationFunctionType, mybir.AxisListType
    ctx = ExitStack()
    with ctx:
        def sb(name, shape, dt=f32):
            return ctx.enter_context(nc.sbuf_tensor(name, shape, dt))

        def sem(name):
            return ctx.enter_context(nc.semaphore(name))

        def hold(eng):
            eng.sem_inc(holds, 1)

        cst = sb("cst", [P, C_N])
        wts = sb("wts", [P, W_N])
        x1_all = sb("x1_all", [P, TOK // P, E])
        x1Th = sb("x1Th", [P, TOK], f32r)
        x1Tl = sb("x1Tl", [P, TOK], f32r)
        wT_all = sb("wT_all", [P, TOK], f32r)
        ident_b = sb("ident_b", [P, P], bf16)
        maskq_b = sb("maskq_b", [P, NW, P], bf16)
        maskt_b = sb("maskt_b", [P, NW, QT], bf16)
        selm_b = sb("selm_b", [P, NG, P], bf16)
        tok_r = sb("tok_r", [4, NT, P], f32r)
        brow = sb("brow", [4, B_N])
        brow_h = sb("brow_h", [4, B_N], f32r)
        brow_r = sb("brow_r", [4, B_N], f32r)
        ones_r = sb("ones_r", [2, SEQ], f32r)
        gb = sb("gb", [P, EXP])
        neg_half = sb("neg_half", [P, 4])
        ident = cst[:, C_ID:C_ID + P]
        head_mask = cst[:, C_HEAD:C_HEAD + HEADS]
        jsel = cst[:, C_J:C_J + EXP + 2]
        c_q, c_k, c_b = (cst[:, C_C + n:C_C + n + 1] for n in range(3))

        xin = sb("xin", [P, 2, NT, E])
        xres = sb("xres", [P, NT, E])
        xT = sb("xT", [P, 2, XW])
        hi4 = sb("hi4", [P, 2 * SEQ], f32r)
        QB = sb("QB", [P, 2, NG, SEQ], f32r)
        KP = sb("KP", [P, 2, NG, XW], f32r)
        V = sb("V", [P, 2, NW, HEADS, 32])
        negm = sb("negm", [P, GH, NG])
        negmb = sb("negmb", [P, GH, 32], bf16)
        negmT = sb("negmT", [P, QT], bf16)
        Pe = sb("Pe", [P, GH, NG, QT])
        cu = sb("cu", [P, NG * QT])
        rec = sb("rec", [P, NG, GH])
        ctxn = sb("ctxn", [P, NG, GH, DH])
        ctxT = sb("ctxT", [P, SEQ])
        cq = sb("cq", [P, 1])
        qblk = sb("qblk", [P, HEADS])
        cqt = sb("cqt", [P, HEADS])
        cmax = sb("cmax", [HEADS, 2])
        ca = sb("ca", [HEADS, SEQ])
        csum = sb("csum", [HEADS, 2])
        cat = sb("cat", [P, NT, HEADS])
        cxb = sb("cxb", [P, HEADS])
        cmm = sb("cmm", [P, HEADS])
        cctx = sb("cctx", [P, 1])
        cpad = sb("cpad", [P, P])
        rr = sb("rr", [P, NT, E])
        st6 = sb("st6", [P, NT, 6])
        mv = sb("mv", [P, NT, 2])
        veps = sb("veps", [P, NT])
        rstd = sb("rstd", [P, NT])
        x1t = sb("x1t", [P, NT, E])
        x1Tf = sb("x1Tf", [P, SEQ])
        th = sb("th", [P, NT, EXP])
        sg = sb("sg", [P, NT, EXP])
        sc = sb("sc", [P, NT, EXP])
        g8 = sb("g8", [P, NT, NGRP, 8])
        gs = sb("gs", [P, NT, NGRP])
        grank = sb("grank", [P, NT, NGRP])
        gtop = sb("gtop", [P, NT, 8])
        gleft = sb("gleft", [P, NT, NGRP])
        gout = sb("gout", [P, NT, NGRP])
        msk = sb("msk", [P, NT, EXP])
        top = sb("top", [P, NT, 8])
        rep = sb("rep", [P, NT, EXP])
        sel = sb("sel", [P, NT, EXP])
        wun = sb("wun", [P, NT, EXP])
        wsum = sb("wsum", [P, NT])
        wrec = sb("wrec", [P, NT])
        wn = sb("wn", [P, NT, EXP])
        wcat = sb("wcat", [P, NT, 2, EXP], f32r)

        wraw = sb("wraw", [P, 3, 3, P])
        wh = sb("wh", [P, 3, 3, P], f32r)
        wl = sb("wl", [P, 3, 3, P], f32r)
        wsel = sb("wsel", [P, 3, 2, F], f32r)
        SG, SU, H = (V[:].rearrange("p i w h c -> p (i w h c)")[:, NSUB * SUB * n:NSUB * SUB * (n + 1)]
                     .rearrange("p (s n) -> p s n", s=NSUB) for n in range(3))
        hh = sb("hh", [P, 3, NSUB, SUB], f32r)
        hl = sb("hl", [P, 3, NSUB, SUB], f32r)
        YT = sb("YT", [P, NSUB, SUB])
        yr = sb("yr", [P, 4, E])
        yst = sb("yst", [P, 4, 6])
        ymv = sb("ymv", [P, 4, 2])
        yve = sb("yve", [P, 4])
        yrs = sb("yrs", [P, 4])
        yo = sb("yo", [P, 4, E])

        bank = [ctx.enter_context(nc.psum_tensor(f"bank{n}", [P, 512], f32)) for n in range(8)]
        bkF, bkB = bank[0], bank[1]
        S_bk, ST_bk = bank[2:4], bank[4:6]
        bkT, bkC = bank[6], bank[7]
        bkTb = bkT[:].bitcast(bf16)
        G_bk, U_bk, W_bk, Y_bk = bank[0:2], bank[2:4], bank[4:6], bank[6:8]

        ld_c, ld_x, ld_r, cst_ok, pool_c = sem("ld_c"), sem("ld_x"), sem("ld_r"), sem("cst_ok"), sem("pool_c")
        xfree = sem("xfree")
        xT_ps, xT_sb = sem("xT_ps"), sem("xT_sb")
        qk_ps, qk_hi, qk_sb = sem("qk_ps"), sem("qk_hi"), sem("qk_sb")
        v_ps, v_sb = sem("v_ps"), sem("v_sb")
        cu_s, cr_s = sem("cu_s"), sem("cr_s")
        s_ps, smax, m_ps, m_sb = sem("s_ps"), sem("smax"), sem("m_ps"), sem("m_sb")
        st_ps, expd, pv_ps, cn, cT_ps = sem("st_ps"), sem("expd"), sem("pv_ps"), sem("cn"), sem("cT_ps")
        b_ps = sem("b_ps")
        wr_s, poolq = sem("wr_s"), sem("poolq")
        clsP, clsA, clsV = sem("clsP"), sem("clsA"), sem("clsV")
        mb_s, backq = sem("mb_s"), sem("backq")
        o_ps, dveq, var_s, pw_s, x1_s = sem("o_ps"), sem("dveq"), sem("var_s"), sem("pw_s"), sem("x1_s")
        x1T_ps, x1T_sb, g_ps, th_s, wc_s, w_ps, wT_s = (sem(n) for n in (
            "x1T_ps", "x1T_sb", "g_ps", "th_s", "wc_s", "w_ps", "wT_s"))
        x1c_s, x1l_s = sem("x1c_s"), sem("x1l_s")
        holds = sem("holds")
        yq = sem("yq")
        ld_w, wh_s, wl_s, wsel_s = sem("ld_w"), sem("wh_s"), sem("wl_s"), sem("wsel_s")
        g_ps2, u_ps, w_b, sg_s, su_s, h_s, hh_s, hl_s, y_ps = (sem(n) for n in (
            "g_ps2", "u_ps", "w_b", "sg_s", "su_s", "h_s", "hh_s", "hl_s", "y_ps"))
        yT_s, yt_ps, yrr, yvar, ypw, yo_s, st_o = (sem(n) for n in (
            "yT_s", "yt_ps", "yrr", "yvar", "ypw", "yo_s", "st_o"))

        block = ctx.enter_context(nc.Block())

        NQ = 4
        NS = NW * GH
        TRIOS = NPAIR // 3
        ATQ, BKQ = 10, 20

        @block.sync
        def _(sp):
            sp.dma_start(cst[:], consts).then_inc(ld_c, 16)
            sp.dma_start(wts[:], wsmall).then_inc(ld_c, 16)
            sp.dma_start(brow[:], brows).then_inc(ld_c, 16)
            sp.dma_start(gb[:], gbias.partition_broadcast(P)).then_inc(ld_c, 16)
            xv = x.rearrange("(b t p) e -> b p t e", t=NT, p=P)

            def load_x(b, u):
                sp.dma_start(xin[:, u], xv[b]).then_inc(ld_x, 16)

            def load_residual(b):
                sp.wait_ge(xfree, b + 1)
                hold(sp)
                sp.dma_start(xres[:], xv[b]).then_inc(ld_r, 16)

            load_x(0, 0)
            sp.wait_ge(ld_x, 16)
            load_x(1, 1)
            load_residual(0)
            with sp.Fori(0, BATCH // 2 - 1) as i:
                for u in range(2):
                    sp.wait_ge(clsV, 14 * i + 7 * u + 6)
                    hold(sp)
                    load_x(2 * i + 2 + u, u)
                    load_residual(2 * i + 1 + u)
            load_residual(BATCH - 1)

            def load(j, n, pair):
                sp.wait_ge(wl_s, n)
                hold(sp)
                sp.wait_ge(ld_w, 16 * n)
                hold(sp)
                sp.dma_start(wraw[:, (j + 1) % 3], wexp[pair]).then_inc(ld_w, 16)

            ov = out.rearrange("(q t p) e -> q p t e", t=SUB // P, p=P)
            sp.dma_start(wraw[:, 0], wexp[0]).then_inc(ld_w, 16)
            with sp.Fori(0, QUARTERS) as q:
                with sp.Fori(0, TRIOS) as k:
                    for j in range(3):
                        load(j, q * NPAIR + 3 * k + j + 1, 3 * k + j + 1)
                for s in range(NSUB):
                    sp.wait_ge(yo_s, q * NSUB + s + 1)
                    hold(sp)
                    sp.dma_start(ov[q * NSUB + s], yo[:]).then_inc(st_o, 16)
            sp.wait_ge(st_o, 16 * QUARTERS * NSUB + 16)

        @block.gpsimd
        def _(pool):
            pool.memset(ones_r[:].bitcast(f32), 1.0).then_inc(pool_c, 1)
            pool.memset(xT[:], 0.0).then_inc(pool_c, 1)
            pool.memset(KP[:].bitcast(f32), 0.0).then_inc(pool_c, 1)
            pool.memset(V[:], 0.0).then_inc(pool_c, 1)
            pool.memset(negmb[:], 0.0).then_inc(pool_c, 1)
            pool.memset(gtop[:], 3e38).then_inc(pool_c, 1)
            pool.memset(ctxT[:], 0.0).then_inc(pool_c, 1)
            pool.memset(cpad[:], 0.0).then_inc(pool_c, 1)
            pool.memset(neg_half[:], -0.5).then_inc(pool_c, 1)
            pool.sem_inc(x1c_s, 1)
            pool.wait_ge(pool_c, 9)
            pool.memset(V[:, :, :, :, DH:DH + 1], 1.0).then_inc(pool_c, 1)
            pool.wait_ge(pool_c, 10)
            with pool.Fori(0, BATCH) as b:
                pool.wait_ge(var_s, b + 1)
                pool.tensor_tensor(rstd[:], veps[:], neg_half[:, 0:NT], ALU.pow).then_inc(pw_s, 1)
                pool.wait_ge(x1_s, b + 1)
                pool.tensor_copy(x1_all[:, bass.ds(NT * b, NT), :], x1t[:]).then_inc(x1c_s, 1)
                pool.wait_ge(x1T_sb, 2 * b + 2)
                pool.tensor_tensor(x1Tl[:, bass.ds(SEQ * b, SEQ)], x1Tf[:],
                                   x1Th[:, bass.ds(SEQ * b, SEQ)].bitcast(f32),
                                   ALU.subtract).then_inc(x1l_s, 1)

                pool.wait_ge(wr_s, b + 1)
                pool.tensor_tensor(wn[:], wun[:], wrec[:].unsqueeze(2).broadcast_to((P, NT, EXP)),
                                   ALU.mult).then_inc(poolq, 1)
                pool.wait_ge(poolq, 3 * b + 1)
                hold(pool)
                pool.tensor_scalar(wn[:], wn[:], ROUTE_SCALE, None, ALU.mult).then_inc(poolq, 1)
                pool.wait_ge(poolq, 3 * b + 2)
                hold(pool)
                pool.tensor_copy(wcat[:, :, 0], wn[:]).then_inc(poolq, 1)
                pool.wait_ge(poolq, 3 * b + 3)
                pool.tensor_tensor(wcat[:, :, 1], wn[:], wcat[:, :, 0].bitcast(f32), ALU.subtract).then_inc(wc_s, 1)

            def low_part(j, n, pair):
                pool.wait_ge(wh_s, n + 1)
                if pair is not None:
                    pool.tensor_copy(wsel[:, j], jsel[:, bass.ds(2 * pair, 2)].unsqueeze(2)
                                     .broadcast_to((P, 2, F))).then_inc(wsel_s, 1)
                pool.tensor_tensor(wl[:, j], wraw[:, j], wh[:, j].bitcast(f32), ALU.subtract).then_inc(wl_s, 1)

            def low_hidden(j, s, n):
                pool.wait_ge(hh_s, NSUB * n + s + 1)
                pool.tensor_tensor(hl[:, j, s], H[:, s], hh[:, j, s].bitcast(f32),
                                   ALU.subtract).then_inc(hl_s, 1)

            pool.sem_inc(wl_s, 2)
            pool.sem_inc(hl_s, 2)
            low_part(0, 0, None)
            with pool.Fori(0, QUARTERS) as q:
                with pool.Fori(0, TRIOS) as k:
                    for j in range(3):
                        n = q * NPAIR + 3 * k + j
                        low_part((j + 1) % 3, n + 1, 3 * k + j)
                        for s in range(NSUB):
                            low_hidden(j, s, n)
                for s in range(NSUB):
                    pool.wait_ge(yvar, q * NSUB + s + 1)
                    pool.tensor_tensor(yrs[:], yve[:], neg_half[:], ALU.pow).then_inc(ypw, 1)

        @block.scalar
        def _(act):
            act.wait_ge(ld_c, 64)
            act.activation(ident_b[:], ident, ACT.Copy).then_inc(cst_ok, 1)
            act.activation(maskq_b[:].rearrange("p w k -> p (w k)"), cst[:, C_MQ:C_MQ + NW * P], ACT.Copy).then_inc(cst_ok, 1)
            act.activation(maskt_b[:].rearrange("p w k -> p (w k)"), cst[:, C_MT:C_MT + NW * QT], ACT.Copy).then_inc(cst_ok, 1)
            act.activation(selm_b[:].rearrange("p w k -> p (w k)"), cst[:, C_SELM:C_SELM + NG * P], ACT.Copy).then_inc(cst_ok, 1)
            act.activation(tok_r[:].rearrange("p w k -> p (w k)"), cst[0:4, C_TOK:C_TOK + NT * P], ACT.Copy).then_inc(cst_ok, 1)
            act.activation(brow_h[:], brow[:], ACT.Copy).then_inc(cst_ok, 1)
            act.preload_act_table(ACT.Exp)
            act.sem_inc(expd, 2)
            act.sem_inc(cu_s, 1)
            act.sem_inc(cr_s, 1)
            act.sem_inc(th_s, 1)
            act.sem_inc(wT_s, 1)
            act.sem_inc(v_sb, 1)

            def x_rows(b, u):
                act.wait_ge(xT_ps, b + 1)
                act.activation(xT[:, u, WIN:WIN + SEQ], bkF[:, 0:SEQ], ACT.Copy).then_inc(xT_sb, 1)

            def high(b, k):
                act.wait_ge(qk_ps, NQ * b + k + 1)
                act.activation(hi4[:], bkF[:], ACT.Copy).then_inc(qk_hi, 1)

            def values(b, u):
                act.wait_ge(v_ps, b + 1)
                act.activation(V[:, u, :, :, 0:DH],
                               bkF[:, 0:NW * P].rearrange("p (w h d) -> p w h d", w=NW, h=HEADS),
                               ACT.Copy).then_inc(v_sb, 1)

            def max_row(b, t):
                act.wait_ge(m_ps, NW * b + t + 1)
                act.activation(negmT[:, 0:QN[t]], bkTb[:, 0:QN[t]], ACT.Copy).then_inc(m_sb, 1)

            def exps(b, t):
                for r in range(GH):
                    act.wait_ge(st_ps, NS * b + GH * t + r + 1)
                    act.activation(Pe[:, r, :, 0:QN[t]],
                                   ST_bk[r % 2][:, 0:NG * QN[t]].rearrange("p (g q) -> p g q", g=NG),
                                   ACT.Exp, scale=SM_SCALE).then_inc(expd, 1)

            def context(b, t):
                act.wait_ge(pv_ps, NW * b + t + 1)
                act.activation(cu[:, 0:NG * QN[t]], bkC[:, 0:NG * QN[t]], ACT.Copy).then_inc(cu_s, 1)

            def ctx_rows(b, t):
                act.wait_ge(cT_ps, NW * b + t + 1)
                lo = 1 if t == 0 else 0
                act.activation(ctxT[:, QT * t + lo:QT * t + QN[t]], bkT[:, lo:QN[t]],
                               ACT.Copy).then_inc(cr_s, 1)

            def x1_rows(b):
                act.wait_ge(x1T_ps, b + 1)
                act.activation(x1Tf[:], bkB[:, 0:SEQ], ACT.Copy).then_inc(x1T_sb, 1)
                act.activation(x1Th[:, bass.ds(SEQ * b, SEQ)], bkB[:, 0:SEQ], ACT.Copy).then_inc(x1T_sb, 1)

            def gate_tanh(b):
                act.wait_ge(g_ps, b + 1)
                act.activation(th[:].rearrange("p j e -> p (j e)"), bkB[:, 0:NT * EXP], ACT.Tanh,
                               scale=0.5).then_inc(th_s, 1)

            def route_rows(b):
                act.wait_ge(w_ps, b + 1)
                act.activation(wT_all[:, bass.ds(SEQ * b, SEQ)], bkB[:, 0:SEQ], ACT.Copy).then_inc(wT_s, 1)

            def batch(b, u, back, front):
                max_row(b, 0)
                if front:
                    x_rows(b + 1, 1 - u)
                exps(b, 0)
                max_row(b, 1)
                if back:
                    x1_rows(b - 1)
                if front:
                    high(b + 1, 0)
                if back:
                    gate_tanh(b - 1)
                act.wait_ge(clsP, 6 * b + 1)
                act.activation(cq[:], bkB[:, 0:1], ACT.Identity, bias=wts[:, W_BQC:W_BQC + 1]).then_inc(clsA, 1)
                context(b, 0)
                exps(b, 1)
                act.wait_ge(clsV, 7 * b + 3)
                act.activation(ca[:], bkB[0:HEADS, 0:SEQ], ACT.Exp, bias=cmax[:, 1:2], scale=SM_SCALE,
                               accum_out=csum[:, 0:1]).then_inc(clsA, 1)
                if front:
                    high(b + 1, 1)
                context(b, 1)
                ctx_rows(b, 0)
                max_row(b, 2)
                if front:
                    high(b + 1, 2)
                exps(b, 2)
                ctx_rows(b, 1)
                if front:
                    high(b + 1, 3)
                context(b, 2)
                if front:
                    values(b + 1, 1 - u)
                ctx_rows(b, 2)
                if back:
                    route_rows(b - 1)

            x_rows(0, 0)
            for k in range(NQ):
                high(0, k)
            values(0, 0)
            batch(0, 0, False, True)
            with act.Fori(0, BATCH // 2 - 1) as i:
                batch(2 * i + 1, 1, True, True)
                batch(2 * i + 2, 0, True, True)
            batch(BATCH - 1, 1, True, False)
            x1_rows(BATCH - 1)
            gate_tanh(BATCH - 1)
            route_rows(BATCH - 1)

            act.preload_act_table(ACT.Silu)
            act.sem_inc(sg_s, 2)
            act.sem_inc(yT_s, 2)

            def high_part(j, n):
                act.wait_ge(ld_w, 16 * n + 16)
                act.wait_ge(y_ps, NSUB * n + 1)
                act.activation(wh[:, j], wraw[:, j], ACT.Copy).then_inc(wh_s, 1)

            def hidden(s, n):
                act.wait_ge(g_ps2, NSUB * n + s + 1)
                act.wait_ge(su_s, NSUB * n + s + 1)
                act.activation(SG[:, s], G_bk[s][:], ACT.Silu).then_inc(sg_s, 1)

            def high_hidden(j, s, n):
                act.wait_ge(h_s, NSUB * n + s + 3)
                act.activation(hh[:, j, s], H[:, s], ACT.Copy).then_inc(hh_s, 1)

            high_part(0, 0)
            with act.Fori(0, QUARTERS) as q:
                with act.Fori(0, TRIOS) as k:
                    for j in range(3):
                        n = q * NPAIR + 3 * k + j
                        hidden(0, n)
                        high_part((j + 1) % 3, n + 1)
                        hidden(1, n)
                        high_hidden(j, 0, n)
                        high_hidden(j, 1, n)
                for s in range(NSUB):
                    act.wait_ge(y_ps, NSUB * (q + 1) * NPAIR + s + 4)
                    act.activation(YT[:, s], Y_bk[s][:], ACT.Copy).then_inc(yT_s, 1)

        @block.vector
        def _(dve):
            links = {}

            def link(ins, base, chain):
                links[chain] += 1
                ins.then_inc(chain, 1)
                dve.wait_ge(chain, base + links[chain])

            dve.wait_ge(cst_ok, 6)
            dve.scalar_tensor_tensor(brow_r[:], brow_h[:].bitcast(f32), c_b[0:4], brow[:],
                                     ALU.mult, ALU.add).then_inc(cst_ok, 1)
            dve.wait_ge(pool_c, 10)
            dve.sem_inc(smax, 2)
            dve.sem_inc(cn, 1)
            dve.sem_inc(xfree, 1)

            def rows_of(b, k, u):
                dve.wait_ge(qk_hi, NQ * b + k + 1)
                g = 2 * (k % 2)
                dst, c = (QB[:, u, g:g + 2, :], c_q) if k < 2 else (KP[:, u, g:g + 2, WIN:WIN + SEQ], c_k)
                dve.scalar_tensor_tensor(dst, hi4[:].bitcast(f32).rearrange("p (a s) -> p a s", a=2), c,
                                         bkF[:].rearrange("p (a s) -> p a s", a=2),
                                         ALU.mult, ALU.add).then_inc(qk_sb, 1)

            def maxima(b, t):
                n = QN[t]
                for r in range(GH):
                    dve.wait_ge(s_ps, NS * b + GH * t + r + 1)
                    dve.tensor_reduce(negm[0:n, r], S_bk[r % 2][0:n, :].rearrange("p (g k) -> p g k", g=NG),
                                      AX.X, ALU.max, negate=True).then_inc(smax, 1)
                dve.wait_ge(smax, NS * b + GH * (t + 1) + 2)
                link(dve.tensor_copy(negmb[0:n, :, 0:NG], negm[0:n]), ATQ * b, dveq)
                dve.tensor_tensor(negmb[0:n, :, NG:2 * NG], negm[0:n], negmb[0:n, :, 0:NG],
                                  ALU.subtract).then_inc(mb_s, 1)

            def normalise(b, t):
                n = QN[t]
                cv = bkT[0:n, :].rearrange("p (g r c) -> p g r c", g=NG, r=GH)
                dve.wait_ge(b_ps, NW * b + t + 1)
                link(dve.reciprocal(rec[0:n], cv[:, :, :, DH]), ATQ * b, dveq)
                dve.tensor_tensor(ctxn[0:n], cv[:, :, :, 0:DH],
                                  rec[0:n].unsqueeze(3).broadcast_to((n, NG, GH, DH)), ALU.mult).then_inc(cn, 1)

            def residual(b):
                base = BKQ * b
                dve.wait_ge(o_ps, b + 1)
                dve.wait_ge(ld_r, 16 * b + 16)
                dve.tensor_tensor(rr[:].rearrange("p j e -> p (j e)"), bkB[:, 0:NT * E],
                                  xres[:].rearrange("p j e -> p (j e)"), ALU.add).then_inc(xfree, 1)
                dve.wait_ge(xfree, b + 2)
                for j in range(NT):
                    link(dve.bn_stats(st6[:, j], rr[:, j]), base, backq)
                for j in range(NT):
                    hold(dve)
                    link(dve.bn_aggr(mv[:, j], st6[:, j]), base, backq)
                dve.tensor_scalar(veps[:], mv[:, :, 1], EPS, None, ALU.add).then_inc(var_s, 1)

            def norm1(b):
                dve.wait_ge(pw_s, b + 1)
                dve.wait_ge(x1c_s, b + 1)
                for j in range(NT):
                    last = dve.tensor_scalar(x1t[:, j], rr[:, j], mv[:, j, 0:1], rstd[:, j:j + 1],
                                             ALU.subtract, ALU.mult)
                    if j < NT - 1:
                        link(last, BKQ * b, backq)
                last.then_inc(x1_s, 1)

            def group_sums(b):
                base = BKQ * b
                dve.wait_ge(th_s, b + 2)
                link(dve.tensor_scalar(sg[:], th[:], 0.5, 0.5, ALU.mult, ALU.add), base, backq)
                link(dve.tensor_tensor(sc[:], sg[:], gb[:].unsqueeze(1).broadcast_to((P, NT, EXP)), ALU.add), base, backq)
                hold(dve)
                for j in range(NT):
                    for a in range(NGRP):
                        last = dve.max(g8[:, j, a], sc[:, j, GS * a:GS * (a + 1)])
                link(last, base, backq)
                link(dve.tensor_tensor(gs[:], g8[:, :, :, 0], g8[:, :, :, 1], ALU.add), base, backq)

            def keep_groups(b):
                base = BKQ * b
                hold(dve)
                for j in range(NT):
                    last = dve.max(grank[:, j], gs[:, j])
                link(last, base, backq)
                link(dve.tensor_copy(gtop[:, :, 0:TOPG], grank[:, :, 0:TOPG]), base, backq)
                hold(dve)
                for j in range(NT):
                    last = dve.match_replace(gleft[:, j], gtop[:, j], gs[:, j], -3e38)
                link(last, base, backq)
                link(dve.tensor_tensor(gout[:], gleft[:], gs[:], ALU.is_equal), base, backq)
                link(dve.scalar_tensor_tensor(msk[:].rearrange("p j (a s) -> p j a s", a=NGRP),
                                              gout[:].unsqueeze(3).broadcast_to((P, NT, NGRP, GS)), NEG,
                                              sc[:].rearrange("p j (a s) -> p j a s", a=NGRP),
                                              ALU.mult, ALU.add), base, backq)

            def top_experts(b):
                base = BKQ * b
                hold(dve)
                for j in range(NT):
                    last = dve.max(top[:, j], msk[:, j])
                link(last, base, backq)
                hold(dve)
                for j in range(NT):
                    last = dve.match_replace(rep[:, j], top[:, j], msk[:, j], -3e38)
                link(last, base, backq)
                link(dve.tensor_tensor(sel[:], rep[:], msk[:], ALU.not_equal), base, backq)
                link(dve.tensor_tensor(wun[:], sg[:], sel[:], ALU.mult), base, backq)

            def inverse_sums(b):
                base = BKQ * b
                link(dve.reduce_sum(wsum[:], wun[:], AX.X), base, backq)
                link(dve.tensor_scalar(wsum[:], wsum[:], 1e-20, None, ALU.add), base, backq)
                dve.reciprocal(wrec[:], wsum[:]).then_inc(wr_s, 1)

            def cls_max(b):
                dve.wait_ge(clsP, 6 * b + 3)
                link(dve.tensor_reduce(cmax[:, 0:1], bkB[0:HEADS, 0:SEQ], AX.X, ALU.max, negate=True), ATQ * b, dveq)
                dve.tensor_scalar(cmax[:, 1:2], cmax[:, 0:1], SM_SCALE, None, ALU.mult).then_inc(clsV, 1)

            def cls_probs(b):
                dve.wait_ge(clsA, 2 * b + 2)
                link(dve.reciprocal(csum[:, 1:2], csum[:, 0:1]), ATQ * b, dveq)
                dve.tensor_scalar(ca[:], ca[:], csum[:, 1:2], None, ALU.mult).then_inc(clsV, 1)

            def cls_ctx(b):
                dve.wait_ge(clsP, 6 * b + 6)
                link(dve.tensor_tensor(cmm[:], bkB[:, 0:HEADS], head_mask, ALU.mult), ATQ * b, dveq)
                link(dve.reduce_sum(cctx[:], cmm[:], AX.X), ATQ * b, dveq)
                dve.tensor_tensor(cpad[:, 0:1], cctx[:], wts[:, W_BVC:W_BVC + 1], ALU.add).then_inc(clsV, 1)

            def cls_copy(b, k, dst, cols):
                dve.wait_ge(clsP, 6 * b + k)
                dve.tensor_copy(dst, bkB[:, 0:cols]).then_inc(clsV, 1)

            def batch(b, u, back, front):
                links[dveq] = links[backq] = 0
                maxima(b, 0)
                maxima(b, 1)
                if back:
                    residual(b - 1)
                    norm1(b - 1)
                if front:
                    rows_of(b + 1, 0, 1 - u)
                maxima(b, 2)
                dve.wait_ge(clsA, 2 * b + 1)
                dve.tensor_scalar(qblk[:], head_mask, cq[:, 0:1], None, ALU.mult).then_inc(clsV, 1)
                if back:
                    group_sums(b - 1)
                cls_copy(b, 2, cqt[:], HEADS)
                normalise(b, 0)
                cls_max(b)
                if front:
                    rows_of(b + 1, 1, 1 - u)
                cls_probs(b)
                if back:
                    keep_groups(b - 1)
                cls_copy(b, 4, cat[:].rearrange("p j h -> p (j h)"), NT * HEADS)
                if front:
                    rows_of(b + 1, 2, 1 - u)
                cls_copy(b, 5, cxb[:], HEADS)
                normalise(b, 1)
                if back:
                    top_experts(b - 1)
                    inverse_sums(b - 1)
                cls_ctx(b)
                if front:
                    rows_of(b + 1, 3, 1 - u)
                normalise(b, 2)
                assert links[dveq] == ATQ and links[backq] in (0, BKQ), links

            for k in range(NQ):
                rows_of(0, k, 0)
            batch(0, 0, False, True)
            with dve.Fori(0, BATCH // 2 - 1) as i:
                batch(2 * i + 1, 1, True, True)
                batch(2 * i + 2, 0, True, True)
            batch(BATCH - 1, 1, True, False)
            links[backq] = 0
            for part in (residual, norm1, group_sums, keep_groups, top_experts, inverse_sums):
                part(BATCH - 1)

            dve.wait_ge(x1c_s, BATCH + 1)
            dve.sem_inc(su_s, 2)
            dve.sem_inc(h_s, 2)
            dve.sem_inc(yrr, 2)
            dve.sem_inc(st_o, 16)

            def hidden(s, n, routed):
                c = NSUB * n + s
                dve.wait_ge(sg_s, c + 3)
                dve.wait_ge(u_ps, c + 1)
                dve.tensor_tensor(SU[:, s], SG[:, s], U_bk[s][:], ALU.mult).then_inc(su_s, 1)
                dve.wait_ge(su_s, c + 3)
                dve.wait_ge(hl_s, c + 1)
                if routed is None:
                    dve.tensor_copy(H[:, s], SU[:, s]).then_inc(h_s, 1)
                else:
                    dve.wait_ge(w_b, routed + s + 1)
                    dve.tensor_tensor(H[:, s], SU[:, s], W_bk[s][:], ALU.mult).then_inc(h_s, 1)

            YL = 8
            with dve.Fori(0, QUARTERS) as q:
                for s in range(NSUB):
                    hidden(s, q * NPAIR, None)
                for j in (1, 2):
                    for s in range(NSUB):
                        hidden(s, q * NPAIR + j, q * NSUB * (NPAIR - 1) + NSUB * (j - 1))
                with dve.Fori(1, TRIOS) as k:
                    for j in range(3):
                        for s in range(NSUB):
                            hidden(s, q * NPAIR + 3 * k + j,
                                   q * NSUB * (NPAIR - 1) + NSUB * 3 * (k - 1) + NSUB * (j + 2))
                links[yq] = 0
                base = NSUB * YL * q
                for s in range(NSUB):
                    i = q * NSUB + s
                    dve.wait_ge(yt_ps, i + 1)
                    dve.tensor_tensor(yr[:], G_bk[s][:].rearrange("p (t e) -> p t e", e=E),
                                      x1_all[:, bass.ds((SUB // P) * i, SUB // P), :], ALU.add).then_inc(yrr, 1)
                    dve.wait_ge(yrr, i + 3)
                    for t in range(4):
                        link(dve.bn_stats(yst[:, t], yr[:, t]), base, yq)
                    for t in range(4):
                        hold(dve)
                        link(dve.bn_aggr(ymv[:, t], yst[:, t]), base, yq)
                    dve.tensor_scalar(yve[:], ymv[:, :, 1], EPS, None, ALU.add).then_inc(yvar, 1)
                    dve.wait_ge(ypw, i + 1)
                    dve.wait_ge(st_o, 16 * i + 16)
                    for t in range(4):
                        last = dve.tensor_scalar(yo[:, t], yr[:, t], ymv[:, t, 0:1], yrs[:, t:t + 1],
                                                 ALU.subtract, ALU.mult)
                    last.then_inc(yo_s, 1)
                    dve.wait_ge(yo_s, i + 1)

        @block.tensor
        def _(pe):
            def mm(o, a, b_, first, last):
                return pe.matmul(o, a, b_, start=first, stop=last)

            pe.wait_ge(cst_ok, 7)
            pe.wait_ge(pool_c, 10)

            def x_rows(b, u):
                pe.wait_ge(ld_x, 16 * b + 16)
                pe.wait_ge(v_sb, b + 1)
                for j in range(NT):
                    last = pe.transpose(bkF[:, P * j:P * (j + 1)], xin[:, u, j], ident)
                last.then_inc(xT_ps, 1)

            def project(b, u, k):
                if k == 0:
                    pe.wait_ge(xT_sb, b + 1)
                else:
                    pe.wait_ge(qk_sb, NQ * b + k)
                for m in range(2):
                    blk = 2 * k + m
                    o = bkF[:, SEQ * m:SEQ * (m + 1)]
                    mm(o, brow_r[0:2, B_QK + P * blk:B_QK + P * (blk + 1)], ones_r[:], True, False)
                    last = mm(o, wts[:, W_QK + P * blk:W_QK + P * (blk + 1)], xT[:, u, WIN:WIN + SEQ], False, True)
                last.then_inc(qk_ps, 1)

            def values(b, u):
                pe.wait_ge(qk_sb, NQ * b + NQ)
                for t in range(NW):
                    o = bkF[:, P * t:P * (t + 1)]
                    mm(o, ones_r[:, 0:P], brow_r[0:2, B_V:B_V + P], True, False)
                    last = mm(o, xT[:, u, QT * t:QT * t + P], wts[:, W_V:W_V + P], False, True)
                last.then_inc(v_ps, 1)

            def scores(b, u, t):
                n = QN[t]
                for r in range(GH):
                    i = NS * b + GH * t + r
                    pe.wait_ge(smax, i + 1)
                    hold(pe)
                    o = S_bk[r % 2]
                    mm(o[0:n, :].rearrange("p (g k) -> p g k", g=NG), ident_b[0:n, 0:n],
                       maskq_b[0:n, t].unsqueeze(1).broadcast_to((n, NG, P)), True, False)
                    for g in range(NG):
                        last = mm(o[0:n, P * g:P * (g + 1)], QB[32 * r:32 * r + 32, u, g, QT * t:QT * t + n],
                                  KP[32 * r:32 * r + 32, u, g, QT * t:QT * t + P], False, g == NG - 1)
                    last.then_inc(s_ps, 1)

            def max_rows(b, t):
                n = QN[t]
                pe.wait_ge(mb_s, NW * b + t + 1)
                if t != 1:
                    pe.wait_ge(cr_s, NW * b + (1 if t == 0 else 2))
                hold(pe)
                pe.transpose(bkTb[:, 0:n], negmb[0:n].rearrange("p r c -> p (r c)"),
                             ident_b[0:n, 0:n]).then_inc(m_ps, 1)

            def scores_t(b, u, t):
                n = QN[t]
                pe.wait_ge(m_sb, NW * b + t + 1)
                for r in range(GH):
                    pe.wait_ge(expd, NS * b + GH * t + r + 1)
                    o = ST_bk[r % 2]
                    rows = slice(32 * r, 32 * r + 32)
                    mm(o[:, 0:NG * n].rearrange("p (g q) -> p g q", g=NG), ident_b[:],
                       maskt_b[:, t, 0:n].unsqueeze(1).broadcast_to((P, NG, n)), True, False)
                    for g in range(NG):
                        mm(o[:, n * g:n * (g + 1)], selm_b[rows, g], negmT[rows, 0:n], False, False)
                        last = mm(o[:, n * g:n * (g + 1)], KP[rows, u, g, QT * t:QT * t + P],
                                  QB[rows, u, g, QT * t:QT * t + n], False, g == NG - 1)
                    last.then_inc(st_ps, 1)

            def pv(b, u, t):
                n = QN[t]
                pe.wait_ge(cu_s, NW * b + t + 1)
                pe.wait_ge(v_sb, b + 2)
                for r in range(GH):
                    pe.wait_ge(expd, NS * b + GH * t + r + 3)
                    for g in range(NG):
                        last = mm(bkC[32 * r:32 * r + 32, n * g:n * (g + 1)],
                                  V[:, u, t, NG * g + r], Pe[:, r, g, 0:n], True, True)
                last.then_inc(pv_ps, 1)

            def by_queries(b, t):
                n = QN[t]
                pe.wait_ge(cu_s, NW * b + t + 2)
                if t < NW - 1:
                    pe.wait_ge(m_sb, NW * b + t + 2)
                else:
                    pe.wait_ge(cr_s, NW * b + t + 1)
                if n < QT:
                    hold(pe)
                for g in range(NG):
                    last = pe.transpose(bkT[0:n, P * g:P * (g + 1)], cu[:, n * g:n * (g + 1)], ident)
                last.then_inc(b_ps, 1)

            def ctx_t(b, t):
                n = QN[t]
                pe.wait_ge(cn, NW * b + t + 2)
                hold(pe)
                pe.transpose(bkT[:, 0:n], ctxn[0:n].rearrange("p g r d -> p (g r d)"),
                             ident[0:n, 0:n]).then_inc(cT_ps, 1)

            def out_proj(b):
                pe.wait_ge(cr_s, NW * (b + 1) + 1)
                pe.wait_ge(clsV, 7 * b + 7)
                pe.wait_ge(wT_s, b + 1)
                for j in range(NT):
                    o = bkB[:, P * j:P * (j + 1)]
                    mm(o, tok_r[:, j], brow_r[:, B_O:B_O + P], True, False)
                    if j == 0:
                        mm(o, cpad[:], wts[:, W_OC:W_OC + P], False, False)
                    last = mm(o, ctxT[:, P * j:P * (j + 1)], wts[:, W_O:W_O + P], False, True)
                last.then_inc(o_ps, 1)

            def x1_rows(b):
                pe.wait_ge(x1_s, b + 1)
                for j in range(NT):
                    last = pe.transpose(bkB[:, P * j:P * (j + 1)], x1t[:, j], ident)
                last.then_inc(x1T_ps, 1)

            def gate(b):
                pe.wait_ge(x1T_sb, 2 * b + 2)
                for j in range(NT):
                    last = mm(bkB[:, EXP * j:EXP * (j + 1)], x1Tf[:, P * j:P * (j + 1)],
                              wts[:, W_G:W_G + EXP], True, True)
                last.then_inc(g_ps, 1)

            def route_rows(b, cls):
                pe.wait_ge(wc_s, b + 1)
                if cls:
                    pe.wait_ge(clsV, 7 * b + 14)
                for j in range(NT):
                    last = pe.transpose(bkB[:, P * j:P * (j + 1)],
                                        wcat[:, j].bitcast(f32).rearrange("p a e -> p (a e)"), ident)
                last.then_inc(w_ps, 1)

            def cls_q(b, u):
                pe.wait_ge(th_s, b + 1)
                mm(bkB[:, 0:1], wts[:, W_QC:W_QC + P], xT[:, u, WIN:WIN + 1], True, True).then_inc(clsP, 1)

            def cls_qk(b):
                pe.wait_ge(clsV, 7 * b + 1)
                mm(bkB[:, 0:HEADS], wts[:, W_KC:W_KC + P], qblk[:], True, True).then_inc(clsP, 1)

            def cls_scores(b, u):
                pe.wait_ge(clsV, 7 * b + 2)
                mm(bkB[0:HEADS, 0:SEQ], cqt[:], xT[:, u, WIN:WIN + SEQ], True, False)
                mm(bkB[0:HEADS, 0:SEQ], qblk[:], wts[:, W_BKC:W_BKC + 1].broadcast_to((P, SEQ)),
                   False, True).then_inc(clsP, 1)

            def cls_t(b):
                pe.wait_ge(clsV, 7 * b + 4)
                hold(pe)
                for j in range(NT):
                    last = pe.transpose(bkB[:, HEADS * j:HEADS * (j + 1)], ca[:, P * j:P * (j + 1)],
                                        ident[0:HEADS, 0:HEADS])
                last.then_inc(clsP, 1)

            def cls_mean(b, u):
                pe.wait_ge(clsV, 7 * b + 5)
                for j in range(NT):
                    last = mm(bkB[:, 0:HEADS], xin[:, u, j], cat[:, j], j == 0, j == NT - 1)
                last.then_inc(clsP, 1)

            def cls_ctx(b):
                pe.wait_ge(clsV, 7 * b + 6)
                mm(bkB[:, 0:HEADS], wts[:, W_VC:W_VC + P], cxb[:], True, True).then_inc(clsP, 1)

            def batch(b, u, back, front):
                if back:
                    out_proj(b - 1)
                max_rows(b, 0)
                scores(b, u, 1)
                if front:
                    x_rows(b + 1, 1 - u)
                scores_t(b, u, 0)
                max_rows(b, 1)
                if back:
                    x1_rows(b - 1)
                if front:
                    project(b + 1, 1 - u, 0)
                if back:
                    gate(b - 1)
                scores(b, u, 2)
                cls_q(b, u)
                pv(b, u, 0)
                cls_qk(b)
                scores_t(b, u, 1)
                by_queries(b, 0)
                cls_scores(b, u)
                if front:
                    project(b + 1, 1 - u, 1)
                pv(b, u, 1)
                ctx_t(b, 0)
                cls_t(b)
                if front:
                    project(b + 1, 1 - u, 2)
                max_rows(b, 2)
                cls_mean(b, u)
                by_queries(b, 1)
                scores_t(b, u, 2)
                ctx_t(b, 1)
                cls_ctx(b)
                if front:
                    project(b + 1, 1 - u, 3)
                pv(b, u, 2)
                if front:
                    values(b + 1, 1 - u)
                by_queries(b, 2)
                if front:
                    scores(b + 1, 1 - u, 0)
                ctx_t(b, 2)
                if back:
                    route_rows(b - 1, True)

            x_rows(0, 0)
            for k in range(NQ):
                project(0, 0, k)
            values(0, 0)
            scores(0, 0, 0)
            batch(0, 0, False, True)
            with pe.Fori(0, BATCH // 2 - 1) as i:
                batch(2 * i + 1, 1, True, True)
                batch(2 * i + 2, 0, True, True)
            batch(BATCH - 1, 1, True, False)
            out_proj(BATCH - 1)
            x1_rows(BATCH - 1)
            gate(BATCH - 1)
            route_rows(BATCH - 1, False)

            pe.wait_ge(wT_s, BATCH + 1)
            pe.wait_ge(x1l_s, BATCH)
            pe.wait_ge(smax, NS * BATCH + 2)
            pe.wait_ge(cn, NW * BATCH + 1)
            pe.sem_inc(y_ps, 5)

            def gate_up(j, s, q, n, first):
                c = NSUB * n + s
                xs = bass.ds(QTOK * q + SUB * s, SUB)
                pe.wait_ge(sg_s, c + 1)
                if s == 0:
                    pe.wait_ge(wl_s, n + 3)
                if first:
                    pe.wait_ge(yrr, NSUB * q + s + 1)
                mm(G_bk[s][:], wh[:, j, 0], x1Th[:, xs], True, False)
                mm(G_bk[s][:], wh[:, j, 0], x1Tl[:, xs], False, False)
                mm(G_bk[s][:], wl[:, j, 0], x1Th[:, xs], False, True).then_inc(g_ps2, 1)
                pe.wait_ge(su_s, c + 1)
                mm(U_bk[s][:], wh[:, j, 1], x1Th[:, xs], True, False)
                mm(U_bk[s][:], wh[:, j, 1], x1Tl[:, xs], False, False)
                mm(U_bk[s][:], wl[:, j, 1], x1Th[:, xs], False, True).then_inc(u_ps, 1)
                if not first:
                    pe.wait_ge(h_s, c + 1)
                    if s == 0:
                        pe.wait_ge(wsel_s, n)
                    mm(W_bk[s][:], wsel[:, j].rearrange("p a f -> p (a f)"), wT_all[:, xs],
                       True, True).then_inc(w_b, 1)

            def down(j, s, q, n, first, last):
                c = NSUB * n + s
                if first:
                    pe.wait_ge(yT_s, NSUB * q + s + 1)
                pe.wait_ge(hh_s, c + 1)
                mm(Y_bk[s][:], wh[:, j, 2], hh[:, j, s], first, False)
                mm(Y_bk[s][:], wl[:, j, 2], hh[:, j, s], False, False)
                pe.wait_ge(hl_s, c + 3)
                mm(Y_bk[s][:], wh[:, j, 2], hl[:, j, s], False, last).then_inc(y_ps, 1)

            with pe.Fori(0, QUARTERS) as q:
                n0 = q * NPAIR
                for s in range(NSUB):
                    gate_up(0, s, q, n0, True)
                for j in (1, 2):
                    for s in range(NSUB):
                        gate_up(j, s, q, n0 + j, False)
                        down(j - 1, s, q, n0 + j - 1, j == 1, False)
                with pe.Fori(1, TRIOS) as k:
                    for j in range(3):
                        n = q * NPAIR + 3 * k + j
                        for s in range(NSUB):
                            gate_up(j, s, q, n, False)
                            down((j + 2) % 3, s, q, n - 1, False, False)
                for s in range(NSUB):
                    down(2, s, q, n0 + NPAIR - 1, False, True)
                for s in range(NSUB):
                    i = NSUB * q + s
                    pe.wait_ge(yT_s, i + 3)
                    pe.wait_ge(sg_s, NSUB * (n0 + NPAIR) + s + 1)
                    for t in range(SUB // P):
                        last = pe.transpose(G_bk[s][:, P * t:P * (t + 1)], YT[:, s, P * t:P * (t + 1)], ident)
                    last.then_inc(yt_ps, 1)


def layouts(a):
    def f(n):
        return np.ascontiguousarray(np.asarray(a[n]))

    e = E
    wl_, bl = f("L0_attn_in_w_loc"), f("L0_attn_in_b_loc")
    wc, bc = f("L0_attn_in_w_cls"), f("L0_attn_in_b_cls")
    ws = np.zeros((P, W_N), np.float32)
    br = np.zeros((4, B_N), np.float32)
    for part in range(2):
        for g in range(NG):
            for r in range(GH):
                h = NG * g + r
                rows = slice(part * e + DH * h, part * e + DH * (h + 1))
                for c in range(3):
                    at = P * (NG * part + g) + 32 * r + DH * c
                    ws[:, W_QK + at:W_QK + at + DH] = wl_[rows].T
                    br[0:2, B_QK + at:B_QK + at + DH] = bl[rows]
    ws[:, W_V:W_V + P] = wl_[2 * e:].T
    ws[:, W_O:W_O + P] = f("L0_attn_out_w_loc").T
    ws[:, W_OC:W_OC + P] = f("L0_attn_out_w_cls").T
    ws[:, W_QC:W_QC + P] = wc[:e].T
    ws[:, W_KC:W_KC + P] = wc[e:2 * e]
    ws[:, W_VC:W_VC + P] = wc[2 * e:].T
    ws[:, W_G:W_G + EXP] = f("L0_ffn_gate_w").T
    ws[:, W_BQC], ws[:, W_BKC], ws[:, W_BVC] = bc[:e], bc[e:2 * e], bc[2 * e:]
    br[0:2, B_V:B_V + P] = bl[2 * e:]
    br[0:2, B_O:B_O + P] = f("L0_attn_out_b_loc")
    br[2:4, B_O:B_O + P] = f("L0_attn_out_b_cls")
    we = np.zeros((NPAIR + 1, P, 3, P), np.float32)
    for at in (0, NPAIR):
        we[at, :, 0, :F], we[at, :, 1, :F], we[at, :F, 2] = f("L0_ffn_Ws_gate"), f("L0_ffn_Ws_up"), f("L0_ffn_Ws_down")
    for i, n in enumerate(("L0_ffn_We_gate", "L0_ffn_We_up")):
        we[1:NPAIR, :, i] = f(n).reshape(EXP // 2, 2, P, F).transpose(0, 2, 1, 3).reshape(EXP // 2, P, P)
    we[1:NPAIR, :, 2] = f("L0_ffn_We_down").reshape(EXP // 2, P, P)
    return {"x": f("L0_attn_hidden_states").reshape(TOK, E), "wsmall": ws, "brows": br,
            "gbias": f("L0_ffn_gate_bias"), "wexp": we, "consts": constants()}


def constants():
    c = np.zeros((P, C_N), np.float32)
    c[:, C_ID:C_ID + P] = np.eye(P)
    i, j = np.arange(QT)[:, None], np.arange(P)[None]
    for t in range(NW):
        key = QT * t - WIN + j
        ok = (j - i >= 0) & (j - i <= 2 * WIN) & (key >= 1) & (key < SEQ)
        m = np.where(ok, 0.0, NEG)
        c[0:QT, C_MQ + P * t:C_MQ + P * (t + 1)] = m
        c[:, C_MT + QT * t:C_MT + QT * (t + 1)] = m.T
    for r in range(GH):
        for g in range(NG):
            c[32 * r + g, C_SELM + P * g:C_SELM + P * (g + 1)] = 1
            c[32 * r + NG + g, C_SELM + P * g:C_SELM + P * (g + 1)] = 1
    c[np.arange(P), C_HEAD + np.arange(P) // DH] = 1
    c[np.arange(P), C_J + np.arange(P) % EXP] = 1
    c[0:2, C_TOK:C_TOK + NT * P] = 1
    c[0:2, C_TOK] = 0
    c[2:4, C_TOK] = 1
    rep = np.arange(P) % 32 // DH
    c[:, C_C] = np.where(rep == 1, -1, 0)
    c[:, C_C + 1] = np.where(rep == 2, -1, 0)
    c[:4, C_C + 2] = [0, -1, 0, -1]
    return c


def kernel(**inputs):
    import concourse.bacc as _bacc
    from concourse.bass_utils import run_bass_kernel_spmd as _run

    nc = _bacc.Bacc("TRN2", target_bir_lowering=False, num_devices=1)
    arrays = layouts(inputs)
    args = [nc.dram_tensor(f"in_{n}", a.shape, mybir.dt.float32, kind="ExternalInput").ap()
            for n, a in arrays.items()]
    args.append(nc.dram_tensor("out_0", (TOK, E), mybir.dt.float32, kind="ExternalOutput").ap())
    build(nc, *args)
    r = _run(nc, [{f"in_{n}": a for n, a in arrays.items()}], core_ids=[0])
    return r.results[0]["out_0"].reshape(BATCH, SEQ, E)
```

```python
import numpy as np
import concourse.bass as bass
from concourse import mybir
from contextlib import ExitStack

P = 128
BATCH, SEQ, E = 16, 256, 128
HEADS, DH, WIN = 16, 8, 16
NG, GH = 4, 4
TOK = BATCH * SEQ
NT = SEQ // P
QT = P - 2 * WIN
QN = [QT, QT, SEQ - 2 * QT]
NW = len(QN)
XW = QT * (NW - 1) + P
EXP, F, TOPK, NGRP, TOPG = 64, 64, 8, 8, 4
GS = EXP // NGRP
NPAIR = EXP // 2 + 1
QUARTERS = 4
QTOK = TOK // QUARTERS
SUB = 512
NSUB = QTOK // SUB
NEG = -1e30
EPS = 1e-5
ROUTE_SCALE = 2.5
SM_SCALE = 1.0 / float(np.sqrt(DH))

C_ID = 0
C_MQ = C_ID + P
C_MT = C_MQ + NW * P
C_SELM = C_MT + NW * QT
C_HEAD = C_SELM + NG * P
C_J = C_HEAD + HEADS
C_TOK = C_J + EXP + 2
C_C = C_TOK + NT * P
C_N = C_C + 3
B_QK, B_V, B_O, B_N = 0, 8 * P, 9 * P, 10 * P
W_QK = 0
W_V = W_QK + 8 * P
W_O, W_OC, W_QC, W_KC, W_VC = (W_V + P * n for n in range(1, 6))
W_G = W_VC + P
W_BQC, W_BKC, W_BVC = W_G + EXP, W_G + EXP + 1, W_G + EXP + 2
W_N = W_BVC + 1


def build(nc, x, wsmall, brows, gbias, wexp, consts, out):
    f32, f32r, bf16 = mybir.dt.float32, mybir.dt.float32r, mybir.dt.bfloat16
    ALU, ACT, AX = mybir.AluOpType, mybir.ActivationFunctionType, mybir.AxisListType
    ctx = ExitStack()
    with ctx:
        def sb(name, shape, dt=f32):
            return ctx.enter_context(nc.sbuf_tensor(name, shape, dt))

        def sem(name):
            return ctx.enter_context(nc.semaphore(name))

        def hold(eng):
            eng.sem_inc(holds, 1)

        cst = sb("cst", [P, C_N])
        wts = sb("wts", [P, W_N])
        x1_all = sb("x1_all", [P, TOK // P, E])
        x1Th = sb("x1Th", [P, TOK], f32r)
        x1Tl = sb("x1Tl", [P, TOK], f32r)
        wT_all = sb("wT_all", [P, TOK], f32r)
        ident_b = sb("ident_b", [P, P], bf16)
        maskq_b = sb("maskq_b", [P, NW, P], bf16)
        maskt_b = sb("maskt_b", [P, NW, QT], bf16)
        selm_b = sb("selm_b", [P, NG, P], bf16)
        tok_r = sb("tok_r", [4, NT, P], f32r)
        brow = sb("brow", [4, B_N])
        brow_h = sb("brow_h", [4, B_N], f32r)
        brow_r = sb("brow_r", [4, B_N], f32r)
        ones_r = sb("ones_r", [2, SEQ], f32r)
        gb = sb("gb", [P, EXP])
        neg_half = sb("neg_half", [P, 4])
        ident = cst[:, C_ID:C_ID + P]
        head_mask = cst[:, C_HEAD:C_HEAD + HEADS]
        jsel = cst[:, C_J:C_J + EXP + 2]
        c_q, c_k, c_b = (cst[:, C_C + n:C_C + n + 1] for n in range(3))

        xin = sb("xin", [P, 2, NT, E])
        xres = sb("xres", [P, NT, E])
        xT = sb("xT", [P, 2, XW])
        hi4 = sb("hi4", [P, 2 * SEQ], f32r)
        QB = sb("QB", [P, 2, NG, SEQ], f32r)
        KP = sb("KP", [P, 2, NG, XW], f32r)
        V = sb("V", [P, 2, NW, HEADS, 32])
        negm = sb("negm", [P, 2, GH, NG])
        negmb = sb("negmb", [P, GH, 32], bf16)
        negmT = sb("negmT", [P, QT], bf16)
        Pe = sb("Pe", [P, GH, NG, QT])
        cu = sb("cu", [P, NG * QT])
        rec = sb("rec", [P, NG, GH])
        ctxn = sb("ctxn", [P, NG, GH, DH])
        ctxT = sb("ctxT", [P, SEQ])
        cq = sb("cq", [P, 1])
        qblk = sb("qblk", [P, HEADS])
        cqt = sb("cqt", [P, HEADS])
        cmax = sb("cmax", [HEADS, 2])
        ca = sb("ca", [HEADS, SEQ])
        csum = sb("csum", [HEADS, 2])
        cat = sb("cat", [P, NT, HEADS])
        cxb = sb("cxb", [P, HEADS])
        cmm = sb("cmm", [P, HEADS])
        cctx = sb("cctx", [P, 1])
        cpad = sb("cpad", [P, P])
        rr = sb("rr", [P, NT, E])
        st6 = sb("st6", [P, NT, 6])
        mv = sb("mv", [P, NT, 2])
        veps = sb("veps", [P, NT])
        rstd = sb("rstd", [P, NT])
        x1t = sb("x1t", [P, NT, E])
        x1Tf = sb("x1Tf", [P, SEQ])
        th = sb("th", [P, NT, EXP])
        sg = sb("sg", [P, NT, EXP])
        sc = sb("sc", [P, NT, EXP])
        g8 = sb("g8", [P, NT, NGRP, 8])
        gs = sb("gs", [P, NT, NGRP])
        grank = sb("grank", [P, NT, NGRP])
        gtop = sb("gtop", [P, NT, 8])
        gleft = sb("gleft", [P, NT, NGRP])
        gout = sb("gout", [P, NT, NGRP])
        msk = sb("msk", [P, NT, EXP])
        top = sb("top", [P, NT, 8])
        rep = sb("rep", [P, NT, EXP])
        sel = sb("sel", [P, NT, EXP])
        wun = sb("wun", [P, NT, EXP])
        wsum = sb("wsum", [P, NT])
        wrec = sb("wrec", [P, NT])
        wn = sb("wn", [P, NT, EXP])
        wcat = sb("wcat", [P, NT, 2, EXP], f32r)

        wraw = sb("wraw", [P, 3, 3, P])
        wh = sb("wh", [P, 3, 3, P], f32r)
        wl = sb("wl", [P, 3, 3, P], f32r)
        wsel = sb("wsel", [P, 3, 2, F], f32r)
        SG, SU, H = (V[:].rearrange("p i w h c -> p (i w h c)")[:, NSUB * SUB * n:NSUB * SUB * (n + 1)]
                     .rearrange("p (s n) -> p s n", s=NSUB) for n in range(3))
        hh = sb("hh", [P, 3, NSUB, SUB], f32r)
        hl = sb("hl", [P, 3, NSUB, SUB], f32r)
        YT = sb("YT", [P, NSUB, SUB])
        ybuf = Pe[:].rearrange("p r g q -> p (r g q)")[:, 0:NSUB * SUB]
        yr = ybuf.rearrange("p (s t e) -> p s t e", s=NSUB, e=E)
        yst = sb("yst", [P, 4, 6])
        ymv = sb("ymv", [P, 4, 2])
        yve = sb("yve", [P, 4])
        yrs = sb("yrs", [P, 4])
        yo = sb("yo", [P, NSUB, 4, E])

        bank = [ctx.enter_context(nc.psum_tensor(f"bank{n}", [P, 512], f32)) for n in range(8)]
        bkF, bkB = bank[0], bank[1]
        S_bk, ST_bk = bank[2:4], bank[4:6]
        bkT, bkC = bank[6], bank[7]
        bkTb = bkT[:].bitcast(bf16)
        G_bk, U_bk, W_bk, Y_bk = (bank[0], bank[2]), (bank[3], bank[4]), (bank[5], bkB), bank[6:8]

        ld_k, ld_c, ld_x, ld_r, cst_ok, pool_c, xfree = (sem(n) for n in (
            "ld_k", "ld_c", "ld_x", "ld_r", "cst_ok", "pool_c", "xfree"))
        xT_ps, xT_sb, qk_ps, qk_hi, qk_sb, v_ps, v_sb = (sem(n) for n in (
            "xT_ps", "xT_sb", "qk_ps", "qk_hi", "qk_sb", "v_ps", "v_sb"))
        s_ps, smax, negm_bf, m_ps, m_sb, attn_link = (sem(n) for n in (
            "s_ps", "smax", "negm_bf", "m_ps", "m_sb", "attn_link"))
        st_ps, expd, pv_ps, ctxu_sb = (sem(n) for n in (
            "st_ps", "expd", "pv_ps", "ctxu_sb"))
        ctxq_ps, ctx_norm, cT_ps, ctxT_sb = (sem(n) for n in (
            "ctxq_ps", "ctx_norm", "cT_ps", "ctxT_sb"))
        clsP, clsA, clsV = (sem(n) for n in (
            "clsP", "clsA", "clsV"))
        o_ps, var_s, pw_s, x1_s, x1c_s, x1T_ps, x1T_sb, x1l_s, back_link = (sem(n) for n in (
            "o_ps", "var_s", "pw_s", "x1_s", "x1c_s", "x1T_ps", "x1T_sb", "x1l_s", "back_link"))
        g_ps, th_s, wrec_s, share_link, wc_s, w_ps, wT_s = (sem(n) for n in (
            "g_ps", "th_s", "wrec_s", "share_link", "wc_s", "w_ps", "wT_s"))
        ld_w, wh_s, wl_s, wsel_s, g_ps2, u_ps, w_b, sg_s, su_s, h_s, hh_s, hl_s, y_ps = (sem(n) for n in (
            "ld_w", "wh_s", "wl_s", "wsel_s", "g_ps2", "u_ps", "w_b", "sg_s", "su_s", "h_s", "hh_s", "hl_s", "y_ps"))
        yT_s, yt_ps, yrr, yvar, ypw, yo_s, st_o, out_link = (sem(n) for n in (
            "yT_s", "yt_ps", "yrr", "yvar", "ypw", "yo_s", "st_o", "out_link"))
        holds = sem("holds")

        block = ctx.enter_context(nc.Block())

        NQ = 4
        NS = NW * GH
        TRIOS = NPAIR // 3
        ATQ, BKQ = 10, 17

        @block.sync
        def _(sp):
            sp.dma_start(cst[:], consts).then_inc(ld_k, 16)
            sp.dma_start(brow[:], brows).then_inc(ld_c, 16)
            sp.dma_start(gb[:], gbias.partition_broadcast(P)).then_inc(ld_c, 16)
            xv = x.rearrange("(b t p) e -> b p t e", t=NT, p=P)

            def load_x(b, u):
                sp.dma_start(xin[:, u], xv[b]).then_inc(ld_x, 16)

            def load_residual(b):
                sp.wait_ge(xfree, b + 1)
                hold(sp)
                sp.dma_start(xres[:], xv[b]).then_inc(ld_r, 16)

            load_x(0, 0)
            sp.dma_start(wts[:], wsmall).then_inc(ld_c, 16)
            sp.wait_ge(ld_x, 16)
            load_x(1, 1)
            sp.dma_start(wraw[:, 0], wexp[0]).then_inc(ld_w, 16)
            load_residual(0)
            with sp.Fori(0, BATCH // 2 - 1) as i:
                for u in range(2):
                    sp.wait_ge(clsV, 14 * i + 7 * u + 6)
                    hold(sp)
                    load_x(2 * i + 2 + u, u)
                    load_residual(2 * i + 1 + u)
            load_residual(BATCH - 1)

            def load(j, n, pair):
                sp.wait_ge(wl_s, n)
                hold(sp)
                sp.wait_ge(ld_w, 16 * n)
                hold(sp)
                sp.dma_start(wraw[:, (j + 1) % 3], wexp[pair]).then_inc(ld_w, 16)

            ov = out.rearrange("(q t p) e -> q p t e", t=SUB // P, p=P)
            def store(q, s):
                i = NSUB * q + s - NSUB
                sp.wait_ge(yo_s, i + 1)
                hold(sp)
                sp.wait_ge(st_o, 16 * i + 32)
                hold(sp)
                sp.dma_start(ov[i], yo[:, s]).then_inc(st_o, 16)

            def load_trio(q, k, stores):
                for j in range(3):
                    load(j, q * NPAIR + 3 * k + j + 1, 3 * k + j + 1)
                    if stores and j < NSUB:
                        store(q, j)

            with sp.Fori(0, TRIOS) as k:
                load_trio(0, k, False)
            with sp.Fori(1, QUARTERS) as q:
                load_trio(q, 0, False)
                load_trio(q, 1, True)
                with sp.Fori(2, TRIOS) as k:
                    load_trio(q, k, False)
            for s in range(NSUB):
                store(QUARTERS, s)
            sp.wait_ge(st_o, 16 * QUARTERS * NSUB + 32)

        @block.gpsimd
        def _(pool):
            pool.memset(ones_r[:].bitcast(f32), 1.0).then_inc(pool_c, 1)
            pool.memset(xT[:], 0.0).then_inc(pool_c, 1)
            pool.memset(KP[:].bitcast(f32), 0.0).then_inc(pool_c, 1)
            pool.memset(V[:], 0.0).then_inc(pool_c, 1)
            pool.memset(negmb[:], 0.0).then_inc(pool_c, 1)
            pool.memset(gtop[:], 3e38).then_inc(pool_c, 1)
            pool.memset(ctxT[:], 0.0).then_inc(pool_c, 1)
            pool.memset(cpad[:], 0.0).then_inc(pool_c, 1)
            pool.memset(neg_half[:], -0.5).then_inc(pool_c, 1)
            pool.sem_inc(x1c_s, 1)
            pool.wait_ge(pool_c, 9)
            pool.memset(V[:, :, :, :, DH:DH + 1], 1.0).then_inc(pool_c, 1)
            pool.wait_ge(pool_c, 10)

            def layernorm1(b):
                pool.wait_ge(var_s, b + 1)
                pool.tensor_tensor(rstd[:], veps[:], neg_half[:, 0:NT], ALU.pow).then_inc(pw_s, 1)
                pool.wait_ge(x1_s, b + 1)
                pool.tensor_copy(x1_all[:, bass.ds(NT * b, NT), :], x1t[:]).then_inc(x1c_s, 1)

            def low_x1(b):
                pool.wait_ge(x1T_sb, 2 * b + 2)
                pool.tensor_tensor(x1Tl[:, bass.ds(SEQ * b, SEQ)], x1Tf[:],
                                   x1Th[:, bass.ds(SEQ * b, SEQ)].bitcast(f32),
                                   ALU.subtract).then_inc(x1l_s, 1)

            def expert_shares(b):
                pool.wait_ge(wrec_s, b + 1)
                pool.tensor_tensor(wn[:], wun[:], wrec[:].unsqueeze(2).broadcast_to((P, NT, EXP)),
                                   ALU.mult).then_inc(share_link, 1)
                pool.wait_ge(share_link, 3 * b + 1)
                hold(pool)
                pool.tensor_scalar(wn[:], wn[:], ROUTE_SCALE, None, ALU.mult).then_inc(share_link, 1)
                pool.wait_ge(share_link, 3 * b + 2)
                hold(pool)
                pool.tensor_copy(wcat[:, :, 0], wn[:]).then_inc(share_link, 1)
                pool.wait_ge(share_link, 3 * b + 3)
                pool.tensor_tensor(wcat[:, :, 1], wn[:], wcat[:, :, 0].bitcast(f32), ALU.subtract).then_inc(wc_s, 1)

            def low_part(j, n):
                pool.wait_ge(wh_s, n + 1)
                pool.tensor_tensor(wl[:, j], wraw[:, j], wh[:, j].bitcast(f32), ALU.subtract).then_inc(wl_s, 1)

            def low_hidden(j, s, n):
                pool.wait_ge(hh_s, NSUB * n + s + 1)
                pool.tensor_tensor(hl[:, j, s], H[:, s], hh[:, j, s].bitcast(f32),
                                   ALU.subtract).then_inc(hl_s, 1)

            with pool.Fori(0, BATCH - 1) as b:
                layernorm1(b)
                low_x1(b)
                expert_shares(b)
            pool.sem_inc(wl_s, 2)
            pool.sem_inc(hl_s, 2)
            low_part(0, 0)
            layernorm1(BATCH - 1)

            def trio(q, k, tail, start=False, divide=False):
                for j in range(3):
                    n = q * NPAIR + 3 * k + j
                    if not (start and j == 0):
                        low_hidden((j + 2) % 3, 1, n - 1)
                    low_part((j + 1) % 3, n + 1)
                    low_hidden(j, 0, n)
                    if start and j == 0:
                        low_x1(BATCH - 1)
                    if divide and j == 0:
                        expert_shares(BATCH - 1)
                    if tail and j > 0:
                        inverse_out(q, j - 1)

            def inverse_out(q, s):
                pool.wait_ge(yvar, NSUB * q + s - NSUB + 1)
                pool.tensor_tensor(yrs[:], yve[:], neg_half[:], ALU.pow).then_inc(ypw, 1)

            trio(0, 0, False, start=True)
            trio(0, 1, False, divide=True)
            with pool.Fori(2, TRIOS) as k:
                trio(0, k, False)
            with pool.Fori(1, QUARTERS) as q:
                trio(q, 0, True)
                with pool.Fori(1, TRIOS) as k:
                    trio(q, k, False)
            low_hidden(2, 1, QUARTERS * NPAIR - 1)
            for s in range(NSUB):
                inverse_out(QUARTERS, s)

        @block.scalar
        def _(act):
            act.wait_ge(ld_k, 16)
            act.activation(ident_b[:], ident, ACT.Copy).then_inc(cst_ok, 1)
            act.activation(maskq_b[:].rearrange("p w k -> p (w k)"), cst[:, C_MQ:C_MQ + NW * P], ACT.Copy).then_inc(cst_ok, 1)
            act.activation(maskt_b[:].rearrange("p w k -> p (w k)"), cst[:, C_MT:C_MT + NW * QT], ACT.Copy).then_inc(cst_ok, 1)
            act.activation(selm_b[:].rearrange("p w k -> p (w k)"), cst[:, C_SELM:C_SELM + NG * P], ACT.Copy).then_inc(cst_ok, 1)
            act.activation(tok_r[:].rearrange("p w k -> p (w k)"), cst[0:4, C_TOK:C_TOK + NT * P], ACT.Copy).then_inc(cst_ok, 1)
            act.wait_ge(ld_c, 48)
            act.activation(brow_h[:], brow[:], ACT.Copy).then_inc(cst_ok, 1)
            act.preload_act_table(ACT.Exp)
            act.sem_inc(expd, 2)
            act.sem_inc(ctxu_sb, 1)
            act.sem_inc(ctxT_sb, 1)
            act.sem_inc(th_s, 1)
            act.sem_inc(wT_s, 1)
            act.sem_inc(v_sb, 1)

            def x_rows(b, u):
                act.wait_ge(xT_ps, b + 1)
                act.activation(xT[:, u, WIN:WIN + SEQ], bkF[:, 0:SEQ], ACT.Copy).then_inc(xT_sb, 1)

            def high(b, k, bk=bkF):
                act.wait_ge(qk_ps, NQ * b + k + 1)
                if k > 0:
                    act.wait_ge(qk_sb, NQ * b + k)
                act.activation(hi4[:], bk[:], ACT.Copy).then_inc(qk_hi, 1)

            def values(b, u):
                act.wait_ge(v_ps, b + 1)
                act.activation(V[:, u, :, :, 0:DH],
                               bkF[:, 0:NW * P].rearrange("p (w h d) -> p w h d", w=NW, h=HEADS),
                               ACT.Copy).then_inc(v_sb, 1)

            def max_row(b, t):
                act.wait_ge(m_ps, NW * b + t + 1)
                act.activation(negmT[:, 0:QN[t]], bkTb[:, 0:QN[t]], ACT.Copy).then_inc(m_sb, 1)

            def exps(b, t, groups=range(GH)):
                for r in groups:
                    act.wait_ge(st_ps, NS * b + GH * t + r + 1)
                    act.activation(Pe[:, r, :, 0:QN[t]],
                                   ST_bk[r % 2][:, 0:NG * QN[t]].rearrange("p (g q) -> p g q", g=NG),
                                   ACT.Exp, scale=SM_SCALE).then_inc(expd, 1)

            def context(b, t):
                act.wait_ge(pv_ps, NW * b + t + 1)
                act.activation(cu[:, 0:NG * QN[t]], bkC[:, 0:NG * QN[t]], ACT.Copy).then_inc(ctxu_sb, 1)

            def ctx_rows(b, t):
                act.wait_ge(cT_ps, NW * b + t + 1)
                lo = 1 if t == 0 else 0
                act.activation(ctxT[:, QT * t + lo:QT * t + QN[t]], bkT[:, lo:QN[t]],
                               ACT.Copy).then_inc(ctxT_sb, 1)

            def x1_rows(b):
                act.wait_ge(x1T_ps, b + 1)
                act.activation(x1Tf[:], bkB[:, 0:SEQ], ACT.Copy).then_inc(x1T_sb, 1)
                act.activation(x1Th[:, bass.ds(SEQ * b, SEQ)], bkB[:, 0:SEQ], ACT.Copy).then_inc(x1T_sb, 1)

            def gate_tanh(b):
                act.wait_ge(g_ps, b + 1)
                act.activation(th[:].rearrange("p j e -> p (j e)"), bkB[:, 0:NT * EXP], ACT.Tanh,
                               scale=0.5).then_inc(th_s, 1)

            def route_rows(b):
                act.wait_ge(w_ps, b + 1)
                act.activation(wT_all[:, bass.ds(SEQ * b, SEQ)], bkB[:, 0:SEQ], ACT.Copy).then_inc(wT_s, 1)

            def batch(b, u, back, front):
                max_row(b, 0)
                if front:
                    x_rows(b + 1, 1 - u)
                exps(b, 0, range(0, 2))
                if front:
                    high(b + 1, 0)
                exps(b, 0, range(2, GH))
                max_row(b, 1)
                if back:
                    x1_rows(b - 1)
                    gate_tanh(b - 1)
                act.wait_ge(clsP, 6 * b + 1)
                act.activation(cq[:], bkB[:, 0:1], ACT.Identity, bias=wts[:, W_BQC:W_BQC + 1]).then_inc(clsA, 1)
                context(b, 0)
                exps(b, 1)
                act.wait_ge(clsV, 7 * b + 3)
                act.activation(ca[:], bkB[0:HEADS, 0:SEQ], ACT.Exp, bias=cmax[:, 1:2], scale=SM_SCALE,
                               accum_out=csum[:, 0:1]).then_inc(clsA, 1)
                if front:
                    high(b + 1, 1)
                context(b, 1)
                ctx_rows(b, 0)
                max_row(b, 2)
                if front:
                    high(b + 1, 2)
                exps(b, 2, range(0, 2))
                if front:
                    high(b + 1, 3)
                exps(b, 2, range(2, GH))
                ctx_rows(b, 1)
                if front:
                    values(b + 1, 1 - u)
                context(b, 2)
                ctx_rows(b, 2)
                if back:
                    route_rows(b - 1)

            act.wait_ge(pool_c, 10)
            x_rows(0, 0)
            for k in range(NQ):
                high(0, k, bank[k])
            values(0, 0)
            batch(0, 0, False, True)
            with act.Fori(0, BATCH // 2 - 1) as i:
                batch(2 * i + 1, 1, True, True)
                batch(2 * i + 2, 0, True, True)
            def high_part(j, n):
                act.wait_ge(ld_w, 16 * n + 16)
                act.wait_ge(y_ps, NSUB * n + 1)
                act.activation(wh[:, j], wraw[:, j], ACT.Copy).then_inc(wh_s, 1)

            high_part(0, 0)
            batch(BATCH - 1, 1, True, False)
            act.preload_act_table(ACT.Silu)
            act.sem_inc(sg_s, 2)
            act.sem_inc(yT_s, 2)

            def hidden(s, n):
                act.wait_ge(g_ps2, NSUB * n + s + 1)
                act.wait_ge(su_s, NSUB * n + s + 1)
                act.activation(SG[:, s], G_bk[s][:], ACT.Silu).then_inc(sg_s, 1)

            def high_hidden(j, s, n):
                act.wait_ge(h_s, NSUB * n + s + 3)
                act.activation(hh[:, j, s], H[:, s], ACT.Copy).then_inc(hh_s, 1)

            def out_rows(q, s):
                act.wait_ge(y_ps, NSUB * q * NPAIR + s + 4)
                act.activation(YT[:, s], Y_bk[s][:], ACT.Copy).then_inc(yT_s, 1)

            def trio(q, k, tail, start=False, route=False):
                for j in range(3):
                    n = q * NPAIR + 3 * k + j
                    hidden(0, n)
                    if tail and j == 0:
                        out_rows(q, 0)
                    if not (start and j == 0):
                        high_hidden((j + 2) % 3, 1, n - 1)
                    high_part((j + 1) % 3, n + 1)
                    hidden(1, n)
                    if start and j < 2:
                        (x1_rows, gate_tanh)[j](BATCH - 1)
                    if tail and j == 0:
                        out_rows(q, 1)
                    high_hidden(j, 0, n)
                    if route and j == 1:
                        route_rows(BATCH - 1)

            trio(0, 0, False, start=True)
            trio(0, 1, False, route=True)
            with act.Fori(2, TRIOS) as k:
                trio(0, k, False)
            with act.Fori(1, QUARTERS) as q:
                trio(q, 0, True)
                with act.Fori(1, TRIOS) as k:
                    trio(q, k, False)
            high_hidden(2, 1, QUARTERS * NPAIR - 1)
            for s in range(NSUB):
                out_rows(QUARTERS, s)

        @block.vector
        def _(dve):
            links = {}

            def link(ins, base, chain):
                links[chain] += 1
                ins.then_inc(chain, 1)
                dve.wait_ge(chain, base + links[chain])

            dve.wait_ge(cst_ok, 6)
            dve.scalar_tensor_tensor(brow_r[:], brow_h[:].bitcast(f32), c_b[0:4], brow[:],
                                     ALU.mult, ALU.add).then_inc(cst_ok, 1)
            dve.wait_ge(pool_c, 10)
            dve.sem_inc(smax, 2)
            dve.sem_inc(ctx_norm, 1)
            dve.sem_inc(xfree, 1)

            def rows_of(b, k, u, bk=bkF):
                dve.wait_ge(qk_hi, NQ * b + k + 1)
                g = 2 * (k % 2)
                dst, c = (QB[:, u, g:g + 2, :], c_q) if k < 2 else (KP[:, u, g:g + 2, WIN:WIN + SEQ], c_k)
                dve.scalar_tensor_tensor(dst, hi4[:].bitcast(f32).rearrange("p (a s) -> p a s", a=2), c,
                                         bk[:].rearrange("p (a s) -> p a s", a=2),
                                         ALU.mult, ALU.add).then_inc(qk_sb, 1)

            def maxima(b, t, groups=range(GH)):
                n = QN[t]
                for r in groups:
                    dve.wait_ge(s_ps, NS * b + GH * t + r + 1)
                    dve.tensor_reduce(negm[0:n, t % 2, r], S_bk[r % 2][0:n, :].rearrange("p (g k) -> p g k", g=NG),
                                      AX.X, ALU.max, negate=True).then_inc(smax, 1)
                if groups[-1] < GH - 1:
                    return
                dve.wait_ge(smax, NS * b + GH * (t + 1) + 2)
                link(dve.tensor_copy(negmb[0:n, :, 0:NG], negm[0:n, t % 2]), ATQ * b, attn_link)
                dve.tensor_tensor(negmb[0:n, :, NG:2 * NG], negm[0:n, t % 2], negmb[0:n, :, 0:NG],
                                  ALU.subtract).then_inc(negm_bf, 1)

            def normalise(b, t):
                n = QN[t]
                cv = bkT[0:n, :].rearrange("p (g r c) -> p g r c", g=NG, r=GH)
                dve.wait_ge(ctxq_ps, NW * b + t + 1)
                link(dve.reciprocal(rec[0:n], cv[:, :, :, DH]), ATQ * b, attn_link)
                dve.tensor_tensor(ctxn[0:n], cv[:, :, :, 0:DH],
                                  rec[0:n].unsqueeze(3).broadcast_to((n, NG, GH, DH)), ALU.mult).then_inc(ctx_norm, 1)

            def residual(b):
                base = BKQ * b
                dve.wait_ge(o_ps, b + 1)
                dve.wait_ge(ld_r, 16 * b + 16)
                dve.tensor_tensor(rr[:].rearrange("p j e -> p (j e)"), bkB[:, 0:NT * E],
                                  xres[:].rearrange("p j e -> p (j e)"), ALU.add).then_inc(xfree, 1)
                dve.wait_ge(xfree, b + 2)
                for j in range(NT):
                    last = dve.bn_stats(st6[:, j], rr[:, j])
                link(last, base, back_link)
                hold(dve)
                for j in range(NT):
                    last = dve.bn_aggr(mv[:, j], st6[:, j])
                link(last, base, back_link)
                dve.tensor_scalar(veps[:], mv[:, :, 1], EPS, None, ALU.add).then_inc(var_s, 1)

            def norm1(b):
                dve.wait_ge(pw_s, b + 1)
                dve.wait_ge(x1c_s, b + 1)
                for j in range(NT):
                    last = dve.tensor_scalar(x1t[:, j], rr[:, j], mv[:, j, 0:1], rstd[:, j:j + 1],
                                             ALU.subtract, ALU.mult)
                last.then_inc(x1_s, 1)

            def group_sums(b):
                base = BKQ * b
                dve.wait_ge(th_s, b + 2)
                link(dve.tensor_scalar(sg[:], th[:], 0.5, 0.5, ALU.mult, ALU.add), base, back_link)
                link(dve.tensor_tensor(sc[:], sg[:], gb[:].unsqueeze(1).broadcast_to((P, NT, EXP)), ALU.add), base, back_link)
                hold(dve)
                for j in range(NT):
                    for a in range(NGRP):
                        last = dve.max(g8[:, j, a], sc[:, j, GS * a:GS * (a + 1)])
                link(last, base, back_link)
                link(dve.tensor_tensor(gs[:], g8[:, :, :, 0], g8[:, :, :, 1], ALU.add), base, back_link)

            def keep_groups(b):
                base = BKQ * b
                hold(dve)
                for j in range(NT):
                    last = dve.max(grank[:, j], gs[:, j])
                link(last, base, back_link)
                link(dve.tensor_copy(gtop[:, :, 0:TOPG], grank[:, :, 0:TOPG]), base, back_link)
                hold(dve)
                for j in range(NT):
                    last = dve.match_replace(gleft[:, j], gtop[:, j], gs[:, j], -3e38)
                link(last, base, back_link)
                link(dve.tensor_tensor(gout[:], gleft[:], gs[:], ALU.is_equal), base, back_link)
                link(dve.scalar_tensor_tensor(msk[:].rearrange("p j (a s) -> p j a s", a=NGRP),
                                              gout[:].unsqueeze(3).broadcast_to((P, NT, NGRP, GS)), NEG,
                                              sc[:].rearrange("p j (a s) -> p j a s", a=NGRP),
                                              ALU.mult, ALU.add), base, back_link)

            def top_experts(b):
                base = BKQ * b
                hold(dve)
                for j in range(NT):
                    last = dve.max(top[:, j], msk[:, j])
                link(last, base, back_link)
                hold(dve)
                for j in range(NT):
                    last = dve.match_replace(rep[:, j], top[:, j], msk[:, j], -3e38)
                link(last, base, back_link)
                link(dve.tensor_tensor(sel[:], rep[:], msk[:], ALU.not_equal), base, back_link)
                link(dve.tensor_tensor(wun[:], sg[:], sel[:], ALU.mult), base, back_link)

            def inverse_sums(b):
                base = BKQ * b
                link(dve.reduce_sum(wsum[:], wun[:], AX.X), base, back_link)
                link(dve.tensor_scalar(wsum[:], wsum[:], 1e-20, None, ALU.add), base, back_link)
                dve.reciprocal(wrec[:], wsum[:]).then_inc(wrec_s, 1)

            def cls_max(b):
                dve.wait_ge(clsP, 6 * b + 3)
                link(dve.tensor_reduce(cmax[:, 0:1], bkB[0:HEADS, 0:SEQ], AX.X, ALU.max, negate=True), ATQ * b, attn_link)
                dve.tensor_scalar(cmax[:, 1:2], cmax[:, 0:1], SM_SCALE, None, ALU.mult).then_inc(clsV, 1)

            def cls_probs(b):
                dve.wait_ge(clsA, 2 * b + 2)
                link(dve.reciprocal(csum[:, 1:2], csum[:, 0:1]), ATQ * b, attn_link)
                dve.tensor_scalar(ca[:], ca[:], csum[:, 1:2], None, ALU.mult).then_inc(clsV, 1)

            def cls_ctx(b):
                dve.wait_ge(clsP, 6 * b + 6)
                link(dve.tensor_tensor(cmm[:], bkB[:, 0:HEADS], head_mask, ALU.mult), ATQ * b, attn_link)
                link(dve.reduce_sum(cctx[:], cmm[:], AX.X), ATQ * b, attn_link)
                dve.tensor_tensor(cpad[:, 0:1], cctx[:], wts[:, W_BVC:W_BVC + 1], ALU.add).then_inc(clsV, 1)

            def cls_copy(b, k, dst, cols):
                dve.wait_ge(clsP, 6 * b + k)
                dve.tensor_copy(dst, bkB[:, 0:cols]).then_inc(clsV, 1)

            def batch(b, u, back, front):
                links[attn_link] = links[back_link] = 0
                maxima(b, 0, range(2, GH))
                maxima(b, 1)
                if back:
                    residual(b - 1)
                    norm1(b - 1)
                if front:
                    rows_of(b + 1, 0, 1 - u)
                maxima(b, 2)
                dve.wait_ge(clsA, 2 * b + 1)
                dve.tensor_scalar(qblk[:], head_mask, cq[:, 0:1], None, ALU.mult).then_inc(clsV, 1)
                if back:
                    group_sums(b - 1)
                cls_copy(b, 2, cqt[:], HEADS)
                normalise(b, 0)
                cls_max(b)
                cls_probs(b)
                if front:
                    rows_of(b + 1, 1, 1 - u)
                if back:
                    keep_groups(b - 1)
                cls_copy(b, 4, cat[:].rearrange("p j h -> p (j h)"), NT * HEADS)
                if front:
                    rows_of(b + 1, 2, 1 - u)
                normalise(b, 1)
                cls_copy(b, 5, cxb[:], HEADS)
                if back:
                    top_experts(b - 1)
                if front:
                    rows_of(b + 1, 3, 1 - u)
                if back:
                    inverse_sums(b - 1)
                cls_ctx(b)
                if front:
                    maxima(b + 1, 0, range(0, 2))
                normalise(b, 2)
                assert links[attn_link] == ATQ and links[back_link] in (0, BKQ), links

            for k in range(NQ):
                rows_of(0, k, 0, bank[k])
            maxima(0, 0, range(0, 2))
            batch(0, 0, False, True)
            with dve.Fori(0, BATCH // 2 - 1) as i:
                batch(2 * i + 1, 1, True, True)
                batch(2 * i + 2, 0, True, True)
            batch(BATCH - 1, 1, True, False)
            links[back_link] = 0
            residual(BATCH - 1)
            dve.sem_inc(su_s, 2)
            dve.sem_inc(h_s, 2)
            dve.sem_inc(yrr, 2)
            dve.sem_inc(st_o, 32)

            def hidden(s, n, routed, alone=False):
                c = NSUB * n + s
                dve.wait_ge(sg_s, c + 3)
                dve.wait_ge(u_ps, c + 1)
                dve.tensor_tensor(SU[:, s], SG[:, s], U_bk[s][:], ALU.mult).then_inc(su_s, 1)
                dve.wait_ge(su_s, c + 3)
                dve.wait_ge(hl_s, c + 1)
                if routed is None:
                    dve.tensor_copy(H[:, s], SU[:, s]).then_inc(h_s, 1)
                else:
                    dve.wait_ge(w_b, routed + s + 1)
                    dve.tensor_tensor(H[:, s], SU[:, s], W_bk[0 if alone else s][:], ALU.mult).then_inc(h_s, 1)

            YL = 2

            def select(j, pair):
                dve.tensor_copy(wsel[:, (j + 1) % 3], jsel[:, bass.ds(2 * pair, 2)].unsqueeze(2)
                                .broadcast_to((P, 2, F))).then_inc(wsel_s, 1)

            def add_x1(q, s):
                i = NSUB * q + s - NSUB
                dve.wait_ge(yt_ps, i + 1)
                dve.tensor_tensor(yr[:, s], W_bk[s][:].rearrange("p (t e) -> p t e", e=E),
                                  x1_all[:, bass.ds((SUB // P) * i, SUB // P), :], ALU.add).then_inc(yrr, 1)

            def statistics(q, s):
                i = NSUB * q + s - NSUB
                links[out_link] = 0
                dve.wait_ge(yrr, i + 3)
                for t in range(SUB // P):
                    last = dve.bn_stats(yst[:, t], yr[:, s, t])
                link(last, YL * i, out_link)
                hold(dve)
                for t in range(SUB // P):
                    last = dve.bn_aggr(ymv[:, t], yst[:, t])
                link(last, YL * i, out_link)
                dve.tensor_scalar(yve[:], ymv[:, :, 1], EPS, None, ALU.add).then_inc(yvar, 1)

            def finish(q, s):
                i = NSUB * q + s - NSUB
                dve.wait_ge(ypw, i + 1)
                dve.wait_ge(st_o, 16 * i + 16)
                for t in range(SUB // P):
                    last = dve.tensor_scalar(yo[:, s, t], yr[:, s, t], ymv[:, t, 0:1], yrs[:, t:t + 1],
                                             ALU.subtract, ALU.mult)
                last.then_inc(yo_s, 1)
                dve.wait_ge(yo_s, i + 1)
                hold(dve)

            def trio(q, k, alone):
                for j in range(3):
                    for s in range(NSUB):
                        hidden(s, q * NPAIR + 3 * k + j,
                               q * NSUB * (NPAIR - 1) + NSUB * 3 * (k - 1) + NSUB * (j + 2), alone)
                        if s == 0:
                            select(j, 3 * k + j)
                        if alone and j == 0 and s == 0:
                            inverse_sums(BATCH - 1)

            def quarter(q, tail):
                if not tail:
                    norm1(BATCH - 1)
                for s in range(NSUB):
                    hidden(s, q * NPAIR, None)
                    if s == 0:
                        select(0, 0)
                if tail:
                    for s in range(NSUB):
                        add_x1(q, s)
                for j in (1, 2):
                    for s in range(NSUB):
                        hidden(s, q * NPAIR + j, q * NSUB * (NPAIR - 1) + NSUB * (j - 1), not tail)
                        if s == 0:
                            select(j, j)
                        if not tail:
                            for part in (((), (group_sums,)), ((keep_groups,), (top_experts,)))[j - 1][s]:
                                part(BATCH - 1)
                        if tail:
                            (statistics, finish)[s](q, j - 1)
                if not tail:
                    trio(q, 1, True)
                with dve.Fori(1 if tail else 2, TRIOS) as k:
                    trio(q, k, False)

            quarter(0, False)
            with dve.Fori(1, QUARTERS) as q:
                quarter(q, True)
            for s in range(NSUB):
                add_x1(QUARTERS, s)
            for s in range(NSUB):
                statistics(QUARTERS, s)
                finish(QUARTERS, s)

        @block.tensor
        def _(pe):
            def mm(o, a, b_, first, last):
                return pe.matmul(o, a, b_, start=first, stop=last)

            pe.sem_inc(y_ps, 5)

            def x_rows(b, u):
                pe.wait_ge(ld_x, 16 * b + 16)
                pe.wait_ge(v_sb, b + 1)
                for j in range(NT):
                    last = pe.transpose(bkF[:, P * j:P * (j + 1)], xin[:, u, j], ident)
                last.then_inc(xT_ps, 1)

            def project(b, u, k, bk=bkF):
                if k == 0 or bk is not bkF:
                    pe.wait_ge(xT_sb, b + 1)
                else:
                    pe.wait_ge(qk_sb, NQ * b + k)
                for m in range(2):
                    blk = 2 * k + m
                    o = bk[:, SEQ * m:SEQ * (m + 1)]
                    mm(o, brow_r[0:2, B_QK + P * blk:B_QK + P * (blk + 1)], ones_r[:], True, False)
                    last = mm(o, wts[:, W_QK + P * blk:W_QK + P * (blk + 1)], xT[:, u, WIN:WIN + SEQ], False, True)
                last.then_inc(qk_ps, 1)

            def values(b, u):
                pe.wait_ge(qk_sb, NQ * b + NQ)
                for t in range(NW):
                    o = bkF[:, P * t:P * (t + 1)]
                    mm(o, ones_r[:, 0:P], brow_r[0:2, B_V:B_V + P], True, False)
                    last = mm(o, xT[:, u, QT * t:QT * t + P], wts[:, W_V:W_V + P], False, True)
                last.then_inc(v_ps, 1)

            def scores(b, u, t, groups=range(GH)):
                n = QN[t]
                for r in groups:
                    i = NS * b + GH * t + r
                    pe.wait_ge(smax, i + 1)
                    hold(pe)
                    o = S_bk[r % 2]
                    mm(o[0:n, :].rearrange("p (g k) -> p g k", g=NG), ident_b[0:n, 0:n],
                       maskq_b[0:n, t].unsqueeze(1).broadcast_to((n, NG, P)), True, False)
                    for g in range(NG):
                        last = mm(o[0:n, P * g:P * (g + 1)], QB[32 * r:32 * r + 32, u, g, QT * t:QT * t + n],
                                  KP[32 * r:32 * r + 32, u, g, QT * t:QT * t + P], False, g == NG - 1)
                    last.then_inc(s_ps, 1)

            def max_rows(b, t):
                n = QN[t]
                pe.wait_ge(negm_bf, NW * b + t + 1)
                if t != 1:
                    pe.wait_ge(ctxT_sb, NW * b + (1 if t == 0 else 2))
                hold(pe)
                pe.transpose(bkTb[:, 0:n], negmb[0:n].rearrange("p r c -> p (r c)"),
                             ident_b[0:n, 0:n]).then_inc(m_ps, 1)

            def scores_t(b, u, t, groups=range(GH)):
                n = QN[t]
                if groups[0] == 0:
                    pe.wait_ge(m_sb, NW * b + t + 1)
                for r in groups:
                    pe.wait_ge(expd, NS * b + GH * t + r + 1)
                    o = ST_bk[r % 2]
                    rows = slice(32 * r, 32 * r + 32)
                    mm(o[:, 0:NG * n].rearrange("p (g q) -> p g q", g=NG), ident_b[:],
                       maskt_b[:, t, 0:n].unsqueeze(1).broadcast_to((P, NG, n)), True, False)
                    for g in range(NG):
                        mm(o[:, n * g:n * (g + 1)], selm_b[rows, g], negmT[rows, 0:n], False, False)
                        last = mm(o[:, n * g:n * (g + 1)], KP[rows, u, g, QT * t:QT * t + P],
                                  QB[rows, u, g, QT * t:QT * t + n], False, g == NG - 1)
                    last.then_inc(st_ps, 1)

            def pv(b, u, t):
                n = QN[t]
                pe.wait_ge(ctxu_sb, NW * b + t + 1)
                pe.wait_ge(v_sb, b + 2)
                for r in range(GH):
                    pe.wait_ge(expd, NS * b + GH * t + r + 3)
                    for g in range(NG):
                        last = mm(bkC[32 * r:32 * r + 32, n * g:n * (g + 1)],
                                  V[:, u, t, NG * g + r], Pe[:, r, g, 0:n], True, True)
                last.then_inc(pv_ps, 1)

            def by_queries(b, t):
                n = QN[t]
                pe.wait_ge(ctxu_sb, NW * b + t + 2)
                if t < NW - 1:
                    pe.wait_ge(m_sb, NW * b + t + 2)
                else:
                    pe.wait_ge(ctxT_sb, NW * b + t + 1)
                if n < QT:
                    hold(pe)
                for g in range(NG):
                    last = pe.transpose(bkT[0:n, P * g:P * (g + 1)], cu[:, n * g:n * (g + 1)], ident)
                last.then_inc(ctxq_ps, 1)

            def ctx_t(b, t):
                n = QN[t]
                pe.wait_ge(ctx_norm, NW * b + t + 2)
                hold(pe)
                pe.transpose(bkT[:, 0:n], ctxn[0:n].rearrange("p g r d -> p (g r d)"),
                             ident[0:n, 0:n]).then_inc(cT_ps, 1)

            def out_proj(b):
                pe.wait_ge(ctxT_sb, NW * (b + 1) + 1)
                pe.wait_ge(clsV, 7 * b + 7)
                pe.wait_ge(wT_s, b + 1)
                for j in range(NT):
                    o = bkB[:, P * j:P * (j + 1)]
                    mm(o, tok_r[:, j], brow_r[:, B_O:B_O + P], True, False)
                    if j == 0:
                        mm(o, cpad[:], wts[:, W_OC:W_OC + P], False, False)
                    last = mm(o, ctxT[:, P * j:P * (j + 1)], wts[:, W_O:W_O + P], False, True)
                last.then_inc(o_ps, 1)

            def x1_rows(b):
                pe.wait_ge(x1_s, b + 1)
                for j in range(NT):
                    last = pe.transpose(bkB[:, P * j:P * (j + 1)], x1t[:, j], ident)
                last.then_inc(x1T_ps, 1)

            def gate(b):
                pe.wait_ge(x1T_sb, 2 * b + 2)
                for j in range(NT):
                    last = mm(bkB[:, EXP * j:EXP * (j + 1)], x1Tf[:, P * j:P * (j + 1)],
                              wts[:, W_G:W_G + EXP], True, True)
                last.then_inc(g_ps, 1)

            def route_rows(b, cls):
                pe.wait_ge(wc_s, b + 1)
                if cls:
                    pe.wait_ge(clsV, 7 * b + 14)
                for j in range(NT):
                    last = pe.transpose(bkB[:, P * j:P * (j + 1)],
                                        wcat[:, j].bitcast(f32).rearrange("p a e -> p (a e)"), ident)
                last.then_inc(w_ps, 1)

            def cls_q(b, u):
                pe.wait_ge(th_s, b + 1)
                mm(bkB[:, 0:1], wts[:, W_QC:W_QC + P], xT[:, u, WIN:WIN + 1], True, True).then_inc(clsP, 1)

            def cls_qk(b):
                pe.wait_ge(clsV, 7 * b + 1)
                mm(bkB[:, 0:HEADS], wts[:, W_KC:W_KC + P], qblk[:], True, True).then_inc(clsP, 1)

            def cls_scores(b, u):
                pe.wait_ge(clsV, 7 * b + 2)
                mm(bkB[0:HEADS, 0:SEQ], cqt[:], xT[:, u, WIN:WIN + SEQ], True, False)
                mm(bkB[0:HEADS, 0:SEQ], qblk[:], wts[:, W_BKC:W_BKC + 1].broadcast_to((P, SEQ)),
                   False, True).then_inc(clsP, 1)

            def cls_t(b):
                pe.wait_ge(clsV, 7 * b + 4)
                hold(pe)
                for j in range(NT):
                    last = pe.transpose(bkB[:, HEADS * j:HEADS * (j + 1)], ca[:, P * j:P * (j + 1)],
                                        ident[0:HEADS, 0:HEADS])
                last.then_inc(clsP, 1)

            def cls_mean(b, u):
                pe.wait_ge(clsV, 7 * b + 5)
                for j in range(NT):
                    last = mm(bkB[:, 0:HEADS], xin[:, u, j], cat[:, j], j == 0, j == NT - 1)
                last.then_inc(clsP, 1)

            def cls_ctx(b):
                pe.wait_ge(clsV, 7 * b + 6)
                mm(bkB[:, 0:HEADS], wts[:, W_VC:W_VC + P], cxb[:], True, True).then_inc(clsP, 1)

            def batch(b, u, back, front):
                scores(b, u, 1, range(0, 2))
                if back:
                    out_proj(b - 1)
                max_rows(b, 0)
                scores(b, u, 1, range(2, GH))
                if front:
                    x_rows(b + 1, 1 - u)
                scores_t(b, u, 0, range(0, 2))
                if front:
                    project(b + 1, 1 - u, 0)
                scores_t(b, u, 0, range(2, GH))
                max_rows(b, 1)
                if back:
                    x1_rows(b - 1)
                scores(b, u, 2, range(0, 2))
                if back:
                    gate(b - 1)
                scores(b, u, 2, range(2, GH))
                cls_q(b, u)
                pv(b, u, 0)
                scores_t(b, u, 1, range(0, 2))
                cls_qk(b)
                by_queries(b, 0)
                scores_t(b, u, 1, range(2, GH))
                cls_scores(b, u)
                if front:
                    project(b + 1, 1 - u, 1)
                pv(b, u, 1)
                ctx_t(b, 0)
                cls_t(b)
                if front:
                    project(b + 1, 1 - u, 2)
                max_rows(b, 2)
                by_queries(b, 1)
                scores_t(b, u, 2, range(0, 1))
                cls_mean(b, u)
                scores_t(b, u, 2, range(1, 2))
                if front:
                    project(b + 1, 1 - u, 3)
                scores_t(b, u, 2, range(2, GH))
                ctx_t(b, 1)
                cls_ctx(b)
                if front:
                    values(b + 1, 1 - u)
                pv(b, u, 2)
                if front:
                    scores(b + 1, 1 - u, 0, range(0, 2))
                by_queries(b, 2)
                if front:
                    scores(b + 1, 1 - u, 0, range(2, GH))
                ctx_t(b, 2)
                if back:
                    route_rows(b - 1, True)

            pe.wait_ge(ld_k, 16)
            x_rows(0, 0)
            pe.wait_ge(cst_ok, 7)
            pe.wait_ge(pool_c, 10)
            for k in range(NQ):
                project(0, 0, k, bank[k])
            values(0, 0)
            scores(0, 0, 0)
            batch(0, 0, False, True)
            with pe.Fori(0, BATCH // 2 - 1) as i:
                batch(2 * i + 1, 1, True, True)
                batch(2 * i + 2, 0, True, True)
            batch(BATCH - 1, 1, True, False)
            out_proj(BATCH - 1)

            pe.wait_ge(x1l_s, BATCH // QUARTERS)
            pe.wait_ge(wT_s, BATCH)
            pe.wait_ge(smax, NS * BATCH + 2)
            pe.wait_ge(ctx_norm, NW * BATCH + 1)

            def gate_up(j, s, q, n):
                c = NSUB * n + s
                xs = bass.ds(QTOK * q + SUB * s, SUB)
                pe.wait_ge(sg_s, c + 1)
                if s == 0:
                    pe.wait_ge(wl_s, n + 3)
                mm(G_bk[s][:], wh[:, j, 0], x1Th[:, xs], True, False)
                mm(G_bk[s][:], wh[:, j, 0], x1Tl[:, xs], False, False)
                mm(G_bk[s][:], wl[:, j, 0], x1Th[:, xs], False, True).then_inc(g_ps2, 1)
                pe.wait_ge(su_s, c + 1)
                mm(U_bk[s][:], wh[:, j, 1], x1Th[:, xs], True, False)
                mm(U_bk[s][:], wh[:, j, 1], x1Tl[:, xs], False, False)
                mm(U_bk[s][:], wl[:, j, 1], x1Th[:, xs], False, True).then_inc(u_ps, 1)

            def shares(j, s, q, n, tail, alone=False):
                o = W_bk[0] if alone else W_bk[s]
                pe.wait_ge(h_s, NSUB * n + s + (2 if alone else 1))
                if s == 0:
                    pe.wait_ge(wsel_s, n)
                if tail:
                    pe.wait_ge(yrr, NSUB * q + s + 1)
                mm(o[:], wsel[:, j].rearrange("p a f -> p (a f)"),
                   wT_all[:, bass.ds(QTOK * q + SUB * s, SUB)], True, True).then_inc(w_b, 1)

            def down(j, s, q, n, first, last):
                c = NSUB * n + s
                if first:
                    pe.wait_ge(yT_s, NSUB * q + s + 1)
                pe.wait_ge(hh_s, c + 1)
                mm(Y_bk[s][:], wh[:, j, 2], hh[:, j, s], first, False)
                mm(Y_bk[s][:], wl[:, j, 2], hh[:, j, s], False, False)
                pe.wait_ge(hl_s, c + 3)
                mm(Y_bk[s][:], wh[:, j, 2], hl[:, j, s], False, last).then_inc(y_ps, 1)

            def by_tokens(q, s):
                pe.wait_ge(yT_s, NSUB * q + s + 1)
                pe.wait_ge(h_s, NSUB * NPAIR * q + s + 1)
                for t in range(SUB // P):
                    last = pe.transpose(W_bk[s][:, P * t:P * (t + 1)], YT[:, s, P * t:P * (t + 1)], ident)
                last.then_inc(yt_ps, 1)

            def trio(q, k, alone):
                for j in range(3):
                    n = q * NPAIR + 3 * k + j
                    for s in range(NSUB):
                        gate_up(j, s, q, n)
                        shares(j, s, q, n, False, alone)
                        down((j + 2) % 3, s, q, n - 1, False, False)
                    if alone and j == 1:
                        route_rows(BATCH - 1, False)

            def quarter(q, tail):
                n0 = q * NPAIR
                for s in range(NSUB):
                    gate_up(0, s, q, n0)
                    if tail:
                        down(2, s, q, n0 - 1, False, True)
                if tail:
                    by_tokens(q, 0)
                else:
                    x1_rows(BATCH - 1)
                for j in (1, 2):
                    for s in range(NSUB):
                        gate_up(j, s, q, n0 + j)
                        if tail and j == 1 and s == 0:
                            by_tokens(q, 1)
                        shares(j, s, q, n0 + j, tail and j == 1, not tail)
                        if not tail and j == 1 and s == 0:
                            gate(BATCH - 1)
                        down(j - 1, s, q, n0 + j - 1, j == 1, False)
                if not tail:
                    trio(q, 1, True)
                    pe.wait_ge(h_s, NSUB * (n0 + 6) + 2)
                    pe.wait_ge(wT_s, BATCH + 1)
                    pe.wait_ge(x1l_s, BATCH)
                with pe.Fori(1 if tail else 2, TRIOS) as k:
                    trio(q, k, False)

            quarter(0, False)
            with pe.Fori(1, QUARTERS) as q:
                quarter(q, True)
            for s in range(NSUB):
                down(2, s, QUARTERS, QUARTERS * NPAIR - 1, False, True)
            for s in range(NSUB):
                by_tokens(QUARTERS, s)


def layouts(a):
    def f(n):
        return np.ascontiguousarray(np.asarray(a[n]))

    e = E
    wl_, bl = f("L0_attn_in_w_loc"), f("L0_attn_in_b_loc")
    wc, bc = f("L0_attn_in_w_cls"), f("L0_attn_in_b_cls")
    ws = np.zeros((P, W_N), np.float32)
    br = np.zeros((4, B_N), np.float32)
    for part in range(2):
        for g in range(NG):
            for r in range(GH):
                h = NG * g + r
                rows = slice(part * e + DH * h, part * e + DH * (h + 1))
                for c in range(3):
                    at = P * (NG * part + g) + 32 * r + DH * c
                    ws[:, W_QK + at:W_QK + at + DH] = wl_[rows].T
                    br[0:2, B_QK + at:B_QK + at + DH] = bl[rows]
    ws[:, W_V:W_V + P] = wl_[2 * e:].T
    ws[:, W_O:W_O + P] = f("L0_attn_out_w_loc").T
    ws[:, W_OC:W_OC + P] = f("L0_attn_out_w_cls").T
    ws[:, W_QC:W_QC + P] = wc[:e].T
    ws[:, W_KC:W_KC + P] = wc[e:2 * e]
    ws[:, W_VC:W_VC + P] = wc[2 * e:].T
    ws[:, W_G:W_G + EXP] = f("L0_ffn_gate_w").T
    ws[:, W_BQC], ws[:, W_BKC], ws[:, W_BVC] = bc[:e], bc[e:2 * e], bc[2 * e:]
    br[0:2, B_V:B_V + P] = bl[2 * e:]
    br[0:2, B_O:B_O + P] = f("L0_attn_out_b_loc")
    br[2:4, B_O:B_O + P] = f("L0_attn_out_b_cls")
    we = np.zeros((NPAIR + 1, P, 3, P), np.float32)
    for at in (0, NPAIR):
        we[at, :, 0, :F], we[at, :, 1, :F], we[at, :F, 2] = f("L0_ffn_Ws_gate"), f("L0_ffn_Ws_up"), f("L0_ffn_Ws_down")
    for i, n in enumerate(("L0_ffn_We_gate", "L0_ffn_We_up")):
        we[1:NPAIR, :, i] = f(n).reshape(EXP // 2, 2, P, F).transpose(0, 2, 1, 3).reshape(EXP // 2, P, P)
    we[1:NPAIR, :, 2] = f("L0_ffn_We_down").reshape(EXP // 2, P, P)
    return {"x": f("L0_attn_hidden_states").reshape(TOK, E), "wsmall": ws, "brows": br,
            "gbias": f("L0_ffn_gate_bias"), "wexp": we, "consts": constants()}


def constants():
    c = np.zeros((P, C_N), np.float32)
    c[:, C_ID:C_ID + P] = np.eye(P)
    i, j = np.arange(QT)[:, None], np.arange(P)[None]
    for t in range(NW):
        key = QT * t - WIN + j
        ok = (j - i >= 0) & (j - i <= 2 * WIN) & (key >= 1) & (key < SEQ)
        m = np.where(ok, 0.0, NEG)
        c[0:QT, C_MQ + P * t:C_MQ + P * (t + 1)] = m
        c[:, C_MT + QT * t:C_MT + QT * (t + 1)] = m.T
    for r in range(GH):
        for g in range(NG):
            c[32 * r + g, C_SELM + P * g:C_SELM + P * (g + 1)] = 1
            c[32 * r + NG + g, C_SELM + P * g:C_SELM + P * (g + 1)] = 1
    c[np.arange(P), C_HEAD + np.arange(P) // DH] = 1
    c[np.arange(P), C_J + np.arange(P) % EXP] = 1
    c[0:2, C_TOK:C_TOK + NT * P] = 1
    c[0:2, C_TOK] = 0
    c[2:4, C_TOK] = 1
    rep = np.arange(P) % 32 // DH
    c[:, C_C] = np.where(rep == 1, -1, 0)
    c[:, C_C + 1] = np.where(rep == 2, -1, 0)
    c[:4, C_C + 2] = [0, -1, 0, -1]
    return c


def kernel(**inputs):
    import concourse.bacc as _bacc
    from concourse.bass_utils import run_bass_kernel_spmd as _run

    nc = _bacc.Bacc("TRN2", target_bir_lowering=False, num_devices=1)
    arrays = layouts(inputs)
    args = [nc.dram_tensor(f"in_{n}", a.shape, mybir.dt.float32, kind="ExternalInput").ap()
            for n, a in arrays.items()]
    args.append(nc.dram_tensor("out_0", (TOK, E), mybir.dt.float32, kind="ExternalOutput").ap())
    build(nc, *args)
    r = _run(nc, [{f"in_{n}": a for n, a in arrays.items()}], core_ids=[0])
    return r.results[0]["out_0"].reshape(BATCH, SEQ, E)
```
